# Optimizing a Trainium2 kernel written in Bass

```python
import numpy as np
import jax
import jax.numpy as jnp

def _softmax(x, axis=-1):
    return jax.nn.softmax(x, axis=axis)

def _gelu(x):
    return jax.nn.gelu(x, approximate=True)

def _silu(x):
    return jax.nn.silu(x)

def _sigmoid(x):
    return jax.nn.sigmoid(x)

def _layernorm(x, axis=-1, eps=1e-05):
    m = jnp.mean(x, axis=axis, keepdims=True)
    v = jnp.var(x, axis=axis, keepdims=True)
    return (x - m) / jnp.sqrt(v + eps)

def _scatter_add(tgt, idx, src, axis=0):
    return tgt.at[idx].add(src)

def _segment_sum(src, seg, n):
    return jax.ops.segment_sum(src, seg, n)
kernel_name = 'mk_gnn_ffn_d1_gnn_r16_893932'

def setup_inputs(seed: int=0):
    np.random.seed(seed)
    _w = jnp.asarray

    def _rec_inputs():
        import jax
        import jax.numpy as jnp
        _gk = jax.random.key(seed)
        x = -0.0003019 + 1 * jax.random.normal(jax.random.fold_in(_gk, 1), (625, 1024), jnp.float32)
        src = jax.random.randint(jax.random.fold_in(_gk, 2), (20000,), 0, 625, jnp.int32)
        dst = jax.random.randint(jax.random.fold_in(_gk, 3), (20000,), 0, 625, jnp.int32)
        _o = jnp.argsort(dst, stable=True)
        src = src[_o]
        dst = dst[_o]
        edge_type_2 = jax.random.randint(jax.random.fold_in(_gk, 12), (20000,), 0, 2, jnp.int32)
        return (x, src, dst, edge_type_2)
    x, src, dst, edge_type_2 = _rec_inputs()

    def _L0_gnn_setup():
        import jax, jax.numpy as jnp
        import numpy as np
        D_MODEL = 1024
        D_FF = 286
        NUM_REL = 2
        EPS = 1e-06

        def t5_layer_norm(x, weight):
            var = jnp.mean(jnp.square(x.astype(jnp.float32)), axis=-1, keepdims=True)
            return weight * (x * jax.lax.rsqrt(var + EPS))

        def rgcn_conv(x, edge_index, edge_type, W_rel, W_root, bias):
            N = x.shape[0]
            src, dst = (edge_index[0], edge_index[1])
            h_src = x[src]
            out = x @ W_root + bias
            for r in range(NUM_REL):
                w = (edge_type == r).astype(x.dtype)
                msg = h_src @ W_rel[r] * w[:, None]
                sums = jax.ops.segment_sum(msg, dst, num_segments=N)
                cnt = jax.ops.segment_sum(w, dst, num_segments=N)
                out = out + sums / jnp.maximum(cnt, 1.0)[:, None]
            return out
        key = jax.random.key(seed)
        ks = jax.random.split(key, 8)
        N, E = (1250, 20000)
        hidden_states = jax.random.normal(ks[0], (N, D_MODEL), dtype=jnp.float32)
        edge_index = jax.random.randint(ks[1], (2, E), 0, N, dtype=jnp.int64)
        edge_type = jax.random.randint(ks[2], (E,), 0, NUM_REL, dtype=jnp.int64)
        ln_weight = jnp.ones((D_MODEL,), dtype=jnp.float32)
        W_rel = jax.random.normal(ks[3], (NUM_REL, D_MODEL, D_FF), dtype=jnp.float32) * (1.0 / np.sqrt(D_MODEL))
        W_root = jax.random.normal(ks[4], (D_MODEL, D_FF), dtype=jnp.float32) * (1.0 / np.sqrt(D_MODEL))
        conv_bias = jnp.zeros((D_FF,), dtype=jnp.float32)
        wo_weight = jax.random.normal(ks[5], (D_FF, D_MODEL), dtype=jnp.float32) * (1.0 / np.sqrt(D_FF))
        return {'hidden_states': hidden_states, 'edge_index': edge_index, 'edge_type': edge_type, 'ln_weight': ln_weight, 'W_rel': W_rel, 'W_root': W_root, 'conv_bias': conv_bias, 'wo_weight': wo_weight}
    _L0_gnn_all = _L0_gnn_setup()
    _L0_gnn_in = {k: v for k, v in _L0_gnn_all.items() if k in ('ln_weight', 'W_rel', 'W_root', 'conv_bias', 'wo_weight')}
    del _L0_gnn_all

    def _L0_ffn_setup():
        import jax, jax.numpy as jnp
        import numpy as np
        D_MODEL = 1024
        HIDDEN = 256
        NUM_EXPERTS = 8
        TOP_K = 2
        NUM_SHARED = 2

        def _gelu(x):
            return jax.nn.gelu(x, approximate=False)
        key = jax.random.key(seed)
        ks = jax.random.split(key, 12)
        s = 0.02
        return {'x': jax.random.normal(ks[0], (2, 128, D_MODEL), dtype=jnp.float32), 'rW': jax.random.normal(ks[1], (D_MODEL, NUM_EXPERTS), dtype=jnp.float32) * s, 'rb': jnp.zeros((NUM_EXPERTS,), dtype=jnp.float32), 'W1': jax.random.normal(ks[2], (NUM_EXPERTS, D_MODEL, HIDDEN), dtype=jnp.float32) * s, 'b1': jnp.zeros((NUM_EXPERTS, HIDDEN), dtype=jnp.float32), 'W2': jax.random.normal(ks[3], (NUM_EXPERTS, HIDDEN, D_MODEL), dtype=jnp.float32) * s, 'b2': jnp.zeros((NUM_EXPERTS, D_MODEL), dtype=jnp.float32), 'sW1': jax.random.normal(ks[4], (NUM_SHARED, D_MODEL, HIDDEN), dtype=jnp.float32) * s, 'sb1': jnp.zeros((NUM_SHARED, HIDDEN), dtype=jnp.float32), 'sW2': jax.random.normal(ks[5], (NUM_SHARED, HIDDEN, D_MODEL), dtype=jnp.float32) * s, 'sb2': jnp.zeros((NUM_SHARED, D_MODEL), dtype=jnp.float32)}
    _L0_ffn_all = _L0_ffn_setup()
    _L0_ffn_in = {k: v for k, v in _L0_ffn_all.items() if k in ('rW', 'rb', 'W1', 'b1', 'W2', 'b2', 'sW1', 'sb1', 'sW2', 'sb2')}
    del _L0_ffn_all
    return {'x': x, 'src': src, 'dst': dst, 'edge_type_2': edge_type_2, 'L0_gnn_ln_weight': _L0_gnn_in['ln_weight'], 'L0_gnn_W_rel': _L0_gnn_in['W_rel'], 'L0_gnn_W_root': _L0_gnn_in['W_root'], 'L0_gnn_conv_bias': _L0_gnn_in['conv_bias'], 'L0_gnn_wo_weight': _L0_gnn_in['wo_weight'], 'L0_ffn_rW': _L0_ffn_in['rW'], 'L0_ffn_rb': _L0_ffn_in['rb'], 'L0_ffn_W1': _L0_ffn_in['W1'], 'L0_ffn_b1': _L0_ffn_in['b1'], 'L0_ffn_W2': _L0_ffn_in['W2'], 'L0_ffn_b2': _L0_ffn_in['b2'], 'L0_ffn_sW1': _L0_ffn_in['sW1'], 'L0_ffn_sb1': _L0_ffn_in['sb1'], 'L0_ffn_sW2': _L0_ffn_in['sW2'], 'L0_ffn_sb2': _L0_ffn_in['sb2']}

def reference(x, src, dst, edge_type_2, L0_gnn_ln_weight, L0_gnn_W_rel, L0_gnn_W_root, L0_gnn_conv_bias, L0_gnn_wo_weight, L0_ffn_rW, L0_ffn_rb, L0_ffn_W1, L0_ffn_b1, L0_ffn_W2, L0_ffn_b2, L0_ffn_sW1, L0_ffn_sb1, L0_ffn_sW2, L0_ffn_sb2):
    import jax
    import jax.numpy as jnp

    def _L0_gnn_ref(hidden_states, edge_index, edge_type, ln_weight, W_rel, W_root, conv_bias, wo_weight):
        import jax, jax.numpy as jnp
        import numpy as np
        D_MODEL = 1024
        D_FF = 286
        NUM_REL = 2
        EPS = 1e-06

        def t5_layer_norm(x, weight):
            var = jnp.mean(jnp.square(x.astype(jnp.float32)), axis=-1, keepdims=True)
            return weight * (x * jax.lax.rsqrt(var + EPS))

        def rgcn_conv(x, edge_index, edge_type, W_rel, W_root, bias):
            N = x.shape[0]
            src, dst = (edge_index[0], edge_index[1])
            h_src = x[src]
            out = x @ W_root + bias
            for r in range(NUM_REL):
                w = (edge_type == r).astype(x.dtype)
                msg = h_src @ W_rel[r] * w[:, None]
                sums = jax.ops.segment_sum(msg, dst, num_segments=N)
                cnt = jax.ops.segment_sum(w, dst, num_segments=N)
                out = out + sums / jnp.maximum(cnt, 1.0)[:, None]
            return out
        norm_x = t5_layer_norm(hidden_states, ln_weight)
        y = jax.nn.elu(rgcn_conv(norm_x, edge_index, edge_type, W_rel, W_root, conv_bias))
        y = y @ wo_weight
        return hidden_states + y

    def _L0_ffn_ref(x, rW, rb, W1, b1, W2, b2, sW1, sb1, sW2, sb2):
        import jax, jax.numpy as jnp
        import numpy as np
        D_MODEL = 1024
        HIDDEN = 256
        NUM_EXPERTS = 8
        TOP_K = 2
        NUM_SHARED = 2

        def _gelu(x):
            return jax.nn.gelu(x, approximate=False)
        B, L, D = x.shape
        xf = x.reshape(-1, D)
        sh = _gelu(jnp.einsum('td,sdh->sth', xf, sW1) + sb1[:, None, :])
        shared = jnp.einsum('sth,shd->std', sh, sW2) + sb2[:, None, :]
        shared = shared.mean(axis=0)
        gates = xf @ rW + rb
        topk_vals, topk_idx = jax.lax.top_k(gates, TOP_K)
        topk_probs = jax.nn.softmax(topk_vals, axis=-1)
        onehot = topk_idx[:, :, None] == jnp.arange(NUM_EXPERTS)[None, None, :]
        w = jnp.sum(topk_probs[:, :, None] * onehot, axis=1)
        h = _gelu(jnp.einsum('td,edh->eth', xf, W1) + b1[:, None, :])
        y = jnp.einsum('eth,ehd->etd', h, W2) + b2[:, None, :]
        moe = jnp.einsum('te,etd->td', w, y)
        return (shared + moe).reshape(B, L, D)
    edge_index = jnp.stack([src, dst])
    x = x + _L0_gnn_ref(_layernorm(x, axis=-1), edge_index, edge_type_2, L0_gnn_ln_weight, L0_gnn_W_rel, L0_gnn_W_root, L0_gnn_conv_bias, L0_gnn_wo_weight)
    x = x + _L0_ffn_ref(_layernorm(x, axis=-1)[None], L0_ffn_rW, L0_ffn_rb, L0_ffn_W1, L0_ffn_b1, L0_ffn_W2, L0_ffn_b2, L0_ffn_sW1, L0_ffn_sb1, L0_ffn_sW2, L0_ffn_sb2)[0]
    return x

_drawn_inputs = setup_inputs


def setup_inputs(seed=0):
    import zlib

    import numpy as np

    out = dict(_drawn_inputs(seed))
    spreads = {'L0_gnn_ln_weight': (1.0, 0.2),
     'L0_gnn_conv_bias': (0.0, 0.1),
     'L0_ffn_rb': (0.0, 0.428),
     'L0_ffn_b1': (0.0, 0.8),
     'L0_ffn_b2': (0.0, 0.1),
     'L0_ffn_sb1': (0.0, 0.8),
     'L0_ffn_sb2': (0.0, 0.1)}
    factors = {}
    for name, (base, spread) in spreads.items():
        noise = np.random.default_rng([zlib.crc32(name.encode()), seed]).standard_normal(out[name].shape)
        drawn = base * np.exp(spread * noise) if base else spread * noise
        out[name] = jnp.asarray(drawn.astype(out[name].dtype))
    for name, factor in factors.items():
        out[name] = (out[name] * factor).astype(out[name].dtype)
    return out
```

```python
import concourse.bass as bass
from concourse import mybir
from contextlib import ExitStack

F32 = mybir.dt.float32
F32R = mybir.dt.float32r
F16 = mybir.dt.float16
I32 = mybir.dt.int32
U32 = mybir.dt.uint32
ALU = mybir.AluOpType
ACT = mybir.ActivationFunctionType
AX = mybir.AxisListType


class Tally:

    def __init__(self, sem):
        self.sem, self.n, self.off = sem, 0, 0

    def mark(self, ins):
        ins.then_inc(self.sem, 1)
        self.n += 1
        return self.n + self.off

    def now(self):
        return self.n + self.off


def window_regs(eng, win, NW, i, u, G):
    at = 2 * i + u
    first = eng.value_load(win[0:1, bass.ds(at, 1)], min_val=0, max_val=G - 1)
    number = eng.value_load(win[0:1, bass.ds(NW + at, 1)], min_val=1, max_val=G)
    before = eng.value_load(win[0:1, bass.ds(2 * NW + at, 1)], min_val=0, max_val=NW * G)
    return first, number, before


def program(nc, x, src, dst, rel, ln_w, w_rel, w_root, conv_b, wo, rw, rb, w1, b1, w2, b2, sw1, sb1, sw2, sb2, out):
    N, D = x.shape
    E = src.shape[0]
    R, _, F = w_rel.shape
    NE, _, HID = w1.shape
    NS = sw1.shape[0]
    NX = NE + NS
    P = 128
    T = -(-N // P)
    rows = [min(P, N - t * P) for t in range(T)]
    KD = D // P
    KH = HID // P
    NP = 628
    NL = NP // 2
    CE = 125
    G = E // (2 * CE)
    KEYS = R * N
    WK = 126
    WD = WK // R
    NW = -(-KEYS // WK)
    ND = NW * WD
    NSRC = N + 1
    NSL = NSRC // 2
    FK = 96
    KF = -(-F // FK)
    frows = [min(FK, F - k * FK) for k in range(KF)]
    DH = D // 2

    ctx = ExitStack()
    with ctx:
        def sb(name, shape, dt=F32):
            return ctx.enter_context(nc.sbuf_tensor(name, shape, dt))

        def sem(name):
            return ctx.enter_context(nc.semaphore(name))

        xt = sb("xt", [P, 2, KD, NP], F32R)
        y_acc = sb("y_acc", [P, T, D])
        ident = sb("ident", [P, P])
        W_REL, W_ROOT, W_O = R * KD * F, KD * F, KF * D
        UNIT = KD * HID
        assert UNIT == KH * D
        arena_r = sb("arena_r", [P, 8 * UNIT + 4 * KH * NP], F32R)
        at = 0

        def cut(n):
            nonlocal at
            at += n
            return arena_r[:, at - n:at]
        rel_hl = [cut(W_REL).rearrange("p (r k f) -> p r k f", r=R, k=KD) for _ in range(2)]
        root_hl = [cut(W_ROOT).rearrange("p (k f) -> p k f", k=KD) for _ in range(2)]
        wo_hl = [cut(W_O).rearrange("p (k n) -> p k n", k=KF) for _ in range(2)]
        yt_hl = [cut(KF * P).rearrange("p (k n) -> p k n", k=KF) for _ in range(2)]
        assert at <= arena_r.shape[1]
        at = 0
        w1_hl = [cut(2 * UNIT).rearrange("p (e k n) -> p e k n", e=2, k=KD) for _ in range(2)]
        w2_hl = [cut(2 * UNIT).rearrange("p (e k n) -> p e k n", e=2, k=KH) for _ in range(2)]
        ht_hl = [cut(2 * KH * NP).rearrange("p (q n) -> p q n", q=2 * KH) for _ in range(2)]
        big = sb("big", [P, max(T * R * ND, NX * NP)])
        h0 = [big[:, i * D:(i + 1) * D] for i in range(2)]
        xn = [big[:, (2 + i) * D:(3 + i) * D] for i in range(2)]
        lnw_row = big[:, 4 * D:5 * D]
        a_t = big[:, 0:T * R * ND].rearrange("p (s r d) -> p s r d", s=T, r=R)
        wb = big[:, 0:NX * NP].rearrange("p (e n) -> p e n", e=NX)
        SLOT = KD * F
        raw = sb("raw", [P, 2 * SLOT])
        slot = [raw[:, i * SLOT:(i + 1) * SLOT] for i in range(2)]
        h_rel = raw[:, 0:T * R * F].rearrange("p (t r f) -> p t r f", t=T, r=R)
        work = sb("work", [P, 2 * D])
        e_int = [work[0:G, i * 250:(i + 1) * 250].bitcast(I32) for i in range(3)]
        key_f = work[0:G, 750:1000]
        src_f = work[0:G, 1000:1250]
        key_hot = [work[0:CE, u * (WK // 2):(u + 1) * (WK // 2)].bitcast(F16) for u in range(2)]
        src_hot = [work[0:CE, WK + u * NSL:WK + (u + 1) * NSL].bitcast(F16) for u in range(2)]
        c_at = WK + 2 * NSL
        cnt_sb = [work[0:WK, c_at + u * NSRC:c_at + (u + 1) * NSRC] for u in range(2)]
        x3 = [work[:, i * D:(i + 1) * D] for i in range(2)]
        g_sb = [work[:, i * NP:(i + 1) * NP] for i in range(2)]
        assert c_at + 2 * NSRC <= 2 * D
        late = sb("late", [P, D])
        iota = late[:, 0:NW * WK // 2].bitcast(F16)
        b2_sb = late[0:NX, :]
        mid = sb("mid", [P, 3 * F])
        z_sb, m_sb, e_sb = (mid[:, i * F:(i + 1) * F] for i in range(3))
        w_t = mid[0:NX, 0:NP]
        key_t = mid[0:CE, 0:2 * G].rearrange("p (j g) -> p j g", j=2)
        src_t = mid[0:CE, 2 * G:4 * G].rearrange("p (j g) -> p j g", j=2)
        diag = mid[0:WK, 4 * G:4 * G + WK]
        bias_row = sb("bias_row", [P, F])
        rw_sb = sb("rw_sb", [P, KD, NE])
        rw_hl = [sb(f"rw_{n}", [P, KD, NE], F32R) for n in ("hi", "lo")]
        rb_row = sb("rb_row", [P, NE])
        b1_rows = sb("b1_rows", [NX * KH, P])
        b1_t = sb("b1_t", [P, NX * KH])
        zeros = sb("zeros", [1, NSRC + WK], F16)
        st = sb("st", [P, 2, 6])
        mv = sb("mv", [P, T, 2])
        rstd = sb("rstd", [P, T])
        minus_half = sb("minus_half", [P, 1])
        nmr = sb("nmr", [P, T])
        sumsq = sb("sumsq", [P, T])
        rms = sb("rms", [P, T])
        kmm = sb("kmm", [G, 2])
        kmm_b = sb("kmm_b", [G, 2, NW])
        first_key = sb("first_key", [NW, 1])
        last_key = sb("last_key", [NW, 1])
        down, up, act_a, act_b = (late[0:NW, D - (i + 1) * G:D - i * G] for i in range(4))
        rng = sb("rng", [NW, 4])
        tri = sb("tri", [NW, NW])
        win = sb("win", [1, 3 * NW], I32)
        cnt = sb("cnt", [WK, 2])
        inv = sb("inv", [WK, 2])
        gate = sb("gate", [P, T, NE])
        top = sb("top", [P, T, 8])
        top_i = sb("top_i", [P, T, 8], U32)
        top_f = sb("top_f", [P, T, 2])
        gd = sb("gd", [P, T])
        ge = sb("ge", [P, T])
        gs = sb("gs", [P, T])
        pr = sb("pr", [P, 2, T])
        hot = sb("hot", [P, 2, T, NE])
        e_idx = sb("e_idx", [P, NE])
        w_sb = sb("w_sb", [P, T, NX])

        ps = [ctx.enter_context(nc.psum_tensor(f"ps{i}", [P, 2, 512], F32)) for i in range(4)]

        def ps_rows(n):
            return ps[n % 2 if n < T else 1][:, :, :].rearrange("p a (b c) -> p (a b) c", c=P)

        s_x = [sem(f"s_xin{t}") for t in range(T)]
        s_edge = sem("s_edge")
        s_lnw = sem("s_lnw")
        s_small = sem("s_small")
        s_b2 = sem("s_b2")
        s_raw = [sem(f"s_raw{i}") for i in range(2)]
        s_const = sem("s_const")
        s_hi = sem("s_hi")
        s_lo = sem("s_lo")
        s_v = sem("s_v")
        s_a = sem("s_a")
        s_kf = sem("s_kf")
        s_kt = sem("s_kt")
        s_rng = sem("s_rng")
        s_rt = sem("s_rt")
        s_win = sem("s_win")
        s_ln = sem("s_ln")
        s_p = sem("s_p")
        s_mv = sem("s_mv")
        s_rms = sem("s_rms")
        s_h0 = sem("s_h0")
        s_xh = sem("s_xh")
        s_n = sem("s_n")
        s_xr = sem("s_xr")
        s_xhi = sem("s_xhi")
        s_xlo = sem("s_xlo")
        s_hot = [sem(f"s_hot{u}") for u in range(2)]
        s_used = [sem(f"s_used{u}") for u in range(2)]
        s_c = sem("s_c")
        s_cs = sem("s_cs")
        s_dgc = sem("s_dgc")
        s_dg = sem("s_dg")
        s_ct = sem("s_ct")
        s_at = sem("s_at")
        s_h = sem("s_h")
        s_hs = sem("s_hs")
        s_agg = sem("s_agg")
        s_m = sem("s_m")
        s_e = sem("s_e")
        s_y = sem("s_y")
        s_yt = sem("s_yt")
        s_yhi = sem("s_yhi")
        s_ylo = sem("s_ylo")
        s_o = sem("s_o")
        s_x2 = sem("s_xtwo")
        s_x3 = sem("s_xthree")
        s_rw = sem("s_rw")
        s_bt = sem("s_bt")
        s_g = sem("s_g")
        s_gd = sem("s_gd")
        s_ge = sem("s_ge")
        s_w = sem("s_w")
        s_wt = sem("s_wt")
        s_wts = sem("s_wts")
        s_wb = sem("s_wb")
        s_wbs = sem("s_wbs")
        f_h = sem("f_h")
        f_g = sem("f_g")
        f_m = sem("f_m")
        f_hi = sem("f_hi")
        f_lo = sem("f_lo")
        f_y = sem("f_y")
        f_acc = sem("f_acc")
        s_out = sem("s_out")

        NG = 5
        NPAIR = NX // 2
        NRP = NE // 2

        def unit(pair, u):
            return NG + 4 * pair + u

        def w_slot(u):
            return (NG + u) % 2

        block = ctx.enter_context(nc.Block())

        @block.sync
        def _(sp):
            def load_x(t):
                sp.dma_start(y_acc[0:rows[t], t, :], x[t * P:t * P + rows[t], :]).then_inc(s_x[t], 16)

            def raw_free(n):
                if not isinstance(n, int) or n >= 2:
                    sp.wait_ge(s_lo, n - 1)

            load_x(0)
            load_x(1)
            sp.dma_start(lnw_row, ln_w.rearrange("(a n) -> a n", a=1).to_broadcast([P, D])).then_inc(s_lnw, 16)
            for t in range(2, T):
                load_x(t)
            for n in range(R):
                sp.dma_start(slot[n].rearrange("p (k f) -> p k f", k=KD),
                             w_rel[n].rearrange("(k p) f -> p k f", p=P)).then_inc(s_raw[n], 16)
            sp.dma_start(bias_row[:, :], conv_b.rearrange("(a n) -> a n", a=1).to_broadcast([P, F])).then_inc(s_lnw, 16)
            raw_free(2)
            sp.dma_start(slot[0].rearrange("p (k f) -> p k f", k=KD),
                         w_root.rearrange("(k p) f -> p k f", p=P)).then_inc(s_raw[0], 16)
            raw_free(3)
            sp.dma_start(slot[1][0:FK, 0:2 * D].rearrange("p (k n) -> p k n", k=2),
                         wo[0:2 * FK, :].rearrange("(k p) n -> p k n", p=FK)).then_inc(s_raw[1], 16)
            raw_free(4)
            sp.dma_start(slot[0][0:frows[2], 0:D], wo[2 * FK:F, :]).then_inc(s_raw[0], 16)
            sp.dma_start(rw_sb[:, :, :], rw.rearrange("(k p) e -> p k e", p=P)).then_inc(s_small, 16)
            sp.dma_start(rb_row[:, :], rb.rearrange("(a n) -> a n", a=1).to_broadcast([P, NE])).then_inc(s_small, 16)
            sp.dma_start(b1_rows[0:NE * KH, :], b1.rearrange("e (m p) -> (e m) p", p=P)).then_inc(s_small, 16)
            sp.dma_start(b1_rows[NE * KH:NX * KH, :], sb1.rearrange("e (m p) -> (e m) p", p=P)).then_inc(s_small, 16)
            sp.wait_ge(s_c, NW)
            sp.dma_start(b2_sb[0:NE, :], b2).then_inc(s_b2, 16)
            sp.dma_start(b2_sb[NE:NX, :], sb2).then_inc(s_b2, 16)
            sp.wait_ge(s_agg, T)

            def load_pair(w1s, w2s, pair):
                for u in range(4):
                    raw_free(unit(pair, u))
                    s = w_slot(u)
                    if u < 2:
                        sp.dma_start(slot[s][:, 0:UNIT].rearrange("p (k n) -> p k n", k=KD),
                                     w1s(u)).then_inc(s_raw[s], 16)
                    else:
                        sp.dma_start(slot[s][:, 0:UNIT].rearrange("p (k n) -> p k n", k=KH),
                                     w2s(u - 2)).then_inc(s_raw[s], 16)

            load_pair(lambda e: sw1[e].rearrange("(k p) n -> p k n", p=P),
                      lambda e: sw2[e].rearrange("(k p) n -> p k n", p=P), 0)
            w1v = w1.rearrange("e (k p) n -> e p k n", p=P)
            w2v = w2.rearrange("e (k p) n -> e p k n", p=P)
            with sp.Fori(0, NRP) as i:
                load_pair(lambda e: w1v[bass.ds(2 * i + e, 1)].rearrange("e p k n -> (e p) k n"),
                          lambda e: w2v[bass.ds(2 * i + e, 1)].rearrange("e p k n -> (e p) k n"), i + 1)
            for t in range(T):
                sp.wait_ge(f_acc, 2 * T * (NPAIR - 1) + 2 * t + 2)
                sp.dma_start(out[t * P:t * P + rows[t], :], y_acc[0:rows[t], t, :]).then_inc(s_out, 16)
            sp.wait_ge(s_out, 16 * T)

        N_CONST = 14

        def kf2(v, n):
            return v.rearrange("p (k n) -> p k n", k=n)
        gnn_units = [(kf2(slot[0], KD), rel_hl[0][:, 0], rel_hl[1][:, 0]),
                     (kf2(slot[1], KD), rel_hl[0][:, 1], rel_hl[1][:, 1]),
                     (kf2(slot[0], KD), root_hl[0], root_hl[1]),
                     (kf2(slot[1][0:FK, 0:2 * D], 2), wo_hl[0][0:FK, 0:2], wo_hl[1][0:FK, 0:2]),
                     (slot[0][0:frows[2], 0:D], wo_hl[0][0:frows[2], 2], wo_hl[1][0:frows[2], 2])]

        @block.gpsimd
        def _(pool):
            k = Tally(s_const)
            k.mark(pool.memset(ident[:, :], 0.0))
            k.mark(pool.memset(tri[:, :], 0.0))
            k.mark(pool.iota(iota, [[1, NW * WK]], base=0, channel_multiplier=0,
                             allow_small_or_imprecise_dtypes=True))
            k.mark(pool.iota(first_key[:, :], [[0, 1]], base=0, channel_multiplier=WK,
                             allow_small_or_imprecise_dtypes=True))
            k.mark(pool.iota(last_key[:, :], [[0, 1]], base=WK - 1, channel_multiplier=WK,
                             allow_small_or_imprecise_dtypes=True))
            k.mark(pool.iota(down, [[-1, G]], base=G, channel_multiplier=0,
                             allow_small_or_imprecise_dtypes=True))
            k.mark(pool.iota(up, [[1, G]], base=1, channel_multiplier=0,
                             allow_small_or_imprecise_dtypes=True))
            k.mark(pool.iota(e_idx[:, :], [[1, NE]], base=0, channel_multiplier=0,
                             allow_small_or_imprecise_dtypes=True))
            k.mark(pool.memset(zeros[:, :], 0.0))
            k.mark(pool.memset(xt[:, :, :, N:NP].bitcast(F32), 0.0))
            k.mark(pool.memset(gate[:, :, :], 0.0))
            k.mark(pool.memset(minus_half[:, :], -0.5))
            pool.wait_ge(s_const, 2)
            k.mark(pool.affine_select(out=ident[:, :], in_=ident[:, :], compare_op=ALU.not_equal, fill=1.0,
                                      base=0, pattern=[[-1, P]], channel_multiplier=1))
            k.mark(pool.affine_select(out=tri[:, :], in_=tri[:, :], compare_op=ALU.is_ge, fill=1.0,
                                      base=0, pattern=[[-1, NW]], channel_multiplier=1))
            assert k.n == N_CONST
            own = Tally(s_p)
            pool.wait_ge(s_const, N_CONST)

            def row_scale(t, n):
                r = rows[t]
                pool.wait_ge(s_mv, n + 1)
                own.mark(pool.tensor_scalar(rstd[0:r, t:t + 1], mv[0:r, t, 1:2], 1.0, 1e-5, ALU.mult, ALU.add))
                pool.wait_ge(s_p, own.n)
                own.mark(pool.tensor_tensor(rstd[0:r, t:t + 1], rstd[0:r, t:t + 1], minus_half[0:r, :], ALU.pow))
                pool.wait_ge(s_p, own.n)
                pool.tensor_scalar(nmr[0:r, t:t + 1], mv[0:r, t, 0:1], rstd[0:r, t:t + 1], -1.0,
                                   ALU.mult, ALU.mult).then_inc(s_ln, 1)

            row_scale(0, 0)
            for t in range(T):
                r = rows[t]
                if t + 1 < T:
                    row_scale(t + 1, t + 1)
                pool.wait_ge(s_h0, t + 1)
                own.mark(pool.tensor_scalar(rms[0:r, t:t + 1], sumsq[0:r, t:t + 1], 1.0 / D, 1e-6,
                                            ALU.mult, ALU.add))
                pool.wait_ge(s_p, own.n)
                pool.tensor_tensor(rms[0:r, t:t + 1], rms[0:r, t:t + 1], minus_half[0:r, :],
                                   ALU.pow).then_inc(s_rms, 1)
                pool.tensor_tensor(y_acc[0:rows[t], t, :], y_acc[0:rows[t], t, :], h0[t % 2][0:rows[t], :],
                                   ALU.add).then_inc(s_xh, 1)
            for n, (raw_v, hi_v, lo_v) in enumerate(gnn_units):
                pool.wait_ge(s_hi, n + 1)
                pool.tensor_tensor(lo_v, raw_v, hi_v.bitcast(F32), ALU.subtract).then_inc(s_lo, 1)
            for t in range(T):
                row_scale(t, T + t)

        def unit_views(u):
            raw_v = slot[w_slot(u)][:, 0:UNIT]
            if u < 2:
                return [kf2(raw_v, KD)] + [w[:, u] for w in w1_hl]
            return [kf2(raw_v, KH)] + [w[:, u - 2] for w in w2_hl]

        def block_of(b):
            return b // 2, b % 2

        @block.scalar
        def _(act):
            v = Tally(s_a)
            for primed in (s_cs, s_at):
                act.sem_inc(primed, 1)
            act.dma_start(e_int[0], dst.rearrange("(p e) -> p e", e=2 * CE)).then_inc(s_edge, 16)
            act.dma_start(e_int[1], rel.rearrange("(p e) -> p e", e=2 * CE)).then_inc(s_edge, 16)
            act.dma_start(e_int[2], src.rearrange("(p e) -> p e", e=2 * CE)).then_inc(s_edge, 16)

            def split_rows(t, n):
                act.wait_ge(s_xr, n + 1)
                act.activation(xt[:, 0, :, t * P:t * P + rows[t]],
                               ps_rows(n)[:, :, 0:rows[t]], ACT.Copy).then_inc(s_xhi, 1)

            for s in range(T + 1):
                if s < T:
                    t, r = s, rows[s]
                    act.wait_ge(s_ln, t + 1)
                    if t >= 2:
                        act.wait_ge(s_xh, t - 1)
                        act.wait_ge(s_xr, t - 1)
                        act.wait_ge(s_n, t - 1)
                    v.mark(act.activation(h0[t % 2][0:r, :], y_acc[0:r, t, :], ACT.Identity,
                                          bias=nmr[0:r, t:t + 1], scale=rstd[0:r, t:t + 1]))
                    act.wait_ge(s_a, v.n)
                    act.activation(xn[t % 2][0:r, :], h0[t % 2][0:r, :], ACT.Square,
                                   accum_out=sumsq[0:r, t:t + 1]).then_inc(s_h0, 1)
                if s >= 1:
                    split_rows(s - 1, s - 1)
            for n, (raw_v, hi_v, lo_v) in enumerate(gnn_units):
                act.wait_ge(s_raw[n % 2], 16 * (n // 2 + 1))
                act.activation(hi_v, raw_v, ACT.Copy).then_inc(s_hi, 1)
            act.wait_ge(s_small, 64)
            act.activation(rw_hl[0][:, :, :], rw_sb[:, :, :], ACT.Copy).then_inc(s_rw, 1)
            act.wait_ge(s_xh, T)
            with act.Fori(0, NW // 2) as i:
                for u in range(2):
                    act.wait_ge(s_c, 2 * i + u + 1)
                    act.wait_ge(s_ct, 2 * i + 1)
                    act.activation(cnt_sb[u].rearrange("p (a n) -> p a n", a=2), ps[u][0:WK, :, 0:NSL], ACT.Copy,
                                   accum_out=cnt[:, u:u + 1]).then_inc(s_cs, 1)
                for u in range(2):
                    act.wait_ge(s_ct, 2 * i + u + 2)
                    dsts = bass.ds(2 * WD * i + u * WD, WD)
                    act.activation(a_t[:, 0:T - 1, :, dsts],
                                   ps[2 + u][:, 0, 0:(T - 1) * WK].rearrange("p (s d r) -> p s r d", s=T - 1, r=R),
                                   ACT.Copy)
                    act.activation(a_t[0:rows[-1], T - 1, :, dsts],
                                   ps[2 + u][0:rows[-1], 1, 0:WK].rearrange("p (d r) -> p r d", r=R),
                                   ACT.Copy).then_inc(s_at, 1)
            act.wait_ge(s_lo, NG)
            for t in range(T):
                act.wait_ge(s_h, t + 1)
                act.activation(h_rel[0:rows[t], t], ps[t % 2][0:rows[t], :, 0:F], ACT.Copy).then_inc(s_hs, 1)
            for s in range(T + 4):
                if s < T:
                    r = rows[s]
                    act.wait_ge(s_m, s + 1)
                    act.activation(e_sb[0:r, :], m_sb[0:r, :], ACT.Exp).then_inc(s_e, 1)
                t = s - 1
                if 0 <= t < T:
                    act.wait_ge(s_yt, t + 1)
                    if t >= 1:
                        act.wait_ge(s_o, t)
                    for k in range(KF):
                        ins = act.activation(yt_hl[0][0:frows[k], k, 0:rows[t]],
                                             ps[2 + t % 2][0:frows[k], 1, k * P:k * P + rows[t]], ACT.Copy)
                    ins.then_inc(s_yhi, 1)
                t = s - 3
                if 0 <= t < T:
                    r = rows[t]
                    act.wait_ge(s_ln, T + t + 1)
                    if t >= 2:
                        act.wait_ge(s_xr, T + t - 1)
                    act.activation(x3[t % 2][0:r, :], y_acc[0:r, t, :], ACT.Identity,
                                   bias=nmr[0:r, t:t + 1], scale=rstd[0:r, t:t + 1]).then_inc(s_x3, 1)
                t = s - 4
                if 0 <= t < T:
                    split_rows(t, T + t)

            def split_hi(pair, u):
                n = unit(pair, u)
                raw_v, hi_v, _ = unit_views(u)
                act.wait_ge(s_raw[w_slot(u)], 16 * ((n - w_slot(u)) // 2 + 1) if isinstance(pair, int)
                            else 16 * ((NG + u - w_slot(u)) // 2 + 1) + 32 * pair)
                if u < 2:
                    act.wait_ge(f_h, 2 * KH * pair)
                else:
                    act.wait_ge(f_y, 2 * T * pair)
                act.activation(hi_v, raw_v, ACT.Copy).then_inc(s_hi, 1)

            split_hi(0, 0)
            split_hi(0, 1)
            act.wait_ge(s_gd, 1)
            act.activation(ge[:, :], gd[:, :], ACT.Exp).then_inc(s_ge, 1)
            act.wait_ge(s_bt, 1)
            act.activation(b1_t[:, :], ps[2][:, 1, 0:NX * KH], ACT.Copy).then_inc(s_rw, 1)
            act.wait_ge(s_rw, 3)

            def hidden(pair, q, first_expert):
                hq = 2 * KH * pair + q
                act.wait_ge(f_h, hq + 1)
                act.wait_ge(f_lo, hq - 1) if not isinstance(hq, int) or hq >= 1 else None
                e = first_expert + q // KH
                col = b1_t[:, bass.ds(e * KH + q % KH, 1)] if not isinstance(e, int) else \
                    b1_t[:, e * KH + q % KH:e * KH + q % KH + 1]
                act.activation(g_sb[q % 2].rearrange("p (a n) -> p a n", a=2), ps[q % 2][:, :, 0:NL],
                               ACT.Gelu, bias=col).then_inc(f_g, 1)

            def hidden_hi(pair, q):
                hq = 2 * KH * pair + q
                act.wait_ge(f_m, hq + 1)
                act.wait_ge(f_y, 2 * T * pair)
                act.activation(ht_hl[0][:, q, :], g_sb[q % 2], ACT.Copy).then_inc(f_hi, 1)

            def pair_act(pair, first_expert, last):
                split_hi(pair, 2)
                hidden(pair, 0, first_expert)
                hidden(pair, 1, first_expert)
                hidden_hi(pair, 0)
                hidden_hi(pair, 1)
                split_hi(pair, 3)
                hidden(pair, 2, first_expert)
                hidden(pair, 3, first_expert)
                hidden_hi(pair, 2)
                hidden_hi(pair, 3)
                if not last:
                    split_hi(pair + 1, 0)
                    split_hi(pair + 1, 1)

            def wb_copy(e):
                act.wait_ge(s_wb, e + 1)
                act.activation(wb[:, e, 0:N], ps[2 + e % 2][:, :, :].rearrange("p a n -> p (a n)")[:, 0:N],
                               ACT.Copy).then_inc(s_wbs, 1)

            pair_act(0, NE, False)
            for e in range(NE):
                wb_copy(e)
            with act.Fori(0, NRP - 1) as i:
                pair_act(i + 1, 2 * i, False)
            pair_act(NRP, 2 * NRP - 2, True)

        @block.vector
        def _(dve):
            v = Tally(s_v)

            def step(ins):
                v.mark(ins)
                dve.wait_ge(s_v, v.n)

            dve.wait_ge(s_const, N_CONST)
            dve.wait_ge(s_edge, 48)
            step(dve.scalar_tensor_tensor(key_f, e_int[0], float(R), e_int[1], ALU.mult, ALU.add))
            step(dve.tensor_copy(src_f, e_int[2]))
            step(dve.tensor_reduce(kmm[:, 0:1], key_f, AX.X, ALU.min))
            step(dve.tensor_reduce(kmm[:, 1:2], key_f, AX.X, ALU.max))
            dve.tensor_copy(kmm_b[:, :, :], kmm[:, :].rearrange("p (a b) -> p a b", b=1)
                            .to_broadcast([G, 2, NW])).then_inc(s_kf, 1)

            def stats(t, n, ready, value):
                r = rows[t]
                dve.wait_ge(ready, value)
                for h in range(2):
                    v.mark(dve.bn_stats(st[0:r, h, :], y_acc[0:r, t, h * 512:(h + 1) * 512]))
                dve.wait_ge(s_v, v.n)
                dve.bn_aggr(mv[0:r, t, :], st[0:r, :, :]).then_inc(s_mv, 1)
                dve.wait_ge(s_mv, n + 1)

            def split_rows_lo(t, n):
                dve.wait_ge(s_xhi, n + 1)
                cols = slice(t * P, t * P + rows[t])
                dve.tensor_tensor(xt[:, 1, :, cols], ps_rows(n)[:, :, 0:rows[t]],
                                  xt[:, 0, :, cols].bitcast(F32), ALU.subtract).then_inc(s_xlo, 1)

            for s in range(T + 2):
                if s < T:
                    stats(s, s, s_x[s], 16)
                t = s - 1
                if 0 <= t < T:
                    r = rows[t]
                    dve.wait_ge(s_rms, t + 1)
                    if t == 0:
                        dve.wait_ge(s_lnw, 32)
                    dve.scalar_tensor_tensor(xn[t % 2][0:r, :], h0[t % 2][0:r, :], rms[0:r, t:t + 1],
                                             lnw_row[0:r, :], ALU.mult, ALU.mult).then_inc(s_n, 1)
                t = s - 2
                if 0 <= t < T:
                    split_rows_lo(t, t)
            dve.wait_ge(s_kt, 1)
            dve.tensor_copy(key_t, ps[2][0:CE, 0, 0:2 * G].rearrange("p (j g) -> p j g", j=2))
            step(dve.tensor_copy(src_t, ps[2][0:CE, 0, 2 * G:4 * G].rearrange("p (j g) -> p j g", j=2)))
            kmin, kmax = ps[3][0:NW, 0, 0:G], ps[3][0:NW, 0, G:2 * G]
            step(dve.tensor_scalar(act_a, kmax, first_key[:, :], None, ALU.is_ge))
            step(dve.scalar_tensor_tensor(act_a, kmin, last_key[:, :], act_a, ALU.is_le, ALU.mult))
            step(dve.tensor_tensor(act_b, act_a, down, ALU.mult))
            step(dve.tensor_tensor(act_a, act_a, up, ALU.mult))
            step(dve.tensor_reduce(rng[:, 0:1], act_b, AX.X, ALU.max))
            step(dve.tensor_reduce(rng[:, 1:2], act_a, AX.X, ALU.max))
            step(dve.tensor_scalar(rng[:, 2:3], rng[:, 0:1], -1.0, float(G), ALU.mult, ALU.add))
            step(dve.tensor_scalar(rng[:, 2:3], rng[:, 2:3], float(G - 1), None, ALU.min))
            step(dve.tensor_tensor(rng[:, 3:4], rng[:, 1:2], rng[:, 2:3], ALU.subtract))
            dve.tensor_scalar(rng[:, 3:4], rng[:, 3:4], 1.0, None, ALU.max).then_inc(s_rng, 1)
            dve.wait_ge(s_rt, 1)
            dve.tensor_copy(win[:, :], ps[3][0:1, 1, 0:3 * NW]).then_inc(s_win, 1)
            dve.wait_ge(s_win, 1)

            with dve.Fori(0, NW // 2) as i:
                for u in range(2):
                    first, number, before = window_regs(dve, win, NW, i, u, G)
                    with dve.Fori(0, number) as j:
                        group = nc.s_assert_within(
                            first + j, 0, G - 1, skip_runtime_bounds_check_because=
                            "first + number is the end of the window's range, at most G whatever the keys are")
                        for c in range(2):
                            dve.wait_ge(s_used[c], before + j + 1)
                            col = bass.ds(group, 1)
                            dve.tensor_scalar(key_hot[c], iota[0:CE, bass.ds(2 * WK * i + WK * u, WK)],
                                              key_t[:, c, col], None, ALU.is_equal)
                            dve.tensor_scalar(src_hot[c], iota[0:CE, 0:NSRC], src_t[:, c, col], None,
                                              ALU.is_equal).then_inc(s_hot[c], 1)
                for u in range(2):
                    dve.wait_ge(s_cs, 2 * i + u + 2)
                    dve.wait_ge(s_ct, 2 * i + u + 1)
                    base = 2 * (2 * i + u)
                    dve.tensor_scalar(cnt[:, u:u + 1], cnt[:, u:u + 1], 1.0, None, ALU.max).then_inc(s_dgc, 1)
                    dve.wait_ge(s_dgc, base + 1)
                    dve.reciprocal(inv[:, u:u + 1], cnt[:, u:u + 1]).then_inc(s_dgc, 1)
                    dve.wait_ge(s_dgc, base + 2)
                    dve.tensor_scalar(diag, ident[0:WK, 0:WK], inv[:, u:u + 1], None,
                                      ALU.mult).then_inc(s_dg, 1)
            dve.wait_ge(s_rw, 1)
            dve.tensor_tensor(rw_hl[1][:, :, :], rw_sb[:, :, :], rw_hl[0][:, :, :].bitcast(F32),
                              ALU.subtract).then_inc(s_rw, 1)
            for s in range(T + 5):
                if s < T:
                    r = rows[s]
                    dve.wait_ge(s_agg, s + 1)
                    if s >= 1:
                        dve.wait_ge(s_yt, s)
                    step(dve.tensor_tensor(z_sb[0:r, :], ps[2 + s % 2][0:r, 0, 0:F], bias_row[0:r, :], ALU.add))
                    dve.tensor_scalar(m_sb[0:r, :], z_sb[0:r, :], 0.0, None, ALU.min).then_inc(s_m, 1)
                    step(dve.tensor_scalar(z_sb[0:r, :], z_sb[0:r, :], 0.0, None, ALU.max))
                    dve.wait_ge(s_e, s + 1)
                    dve.scalar_tensor_tensor(z_sb[0:r, :], e_sb[0:r, :], -1.0, z_sb[0:r, :],
                                             ALU.add, ALU.add).then_inc(s_y, 1)
                t = s - 1
                if 0 <= t < T:
                    dve.wait_ge(s_yhi, t + 1)
                    for k in range(KF):
                        f, r = frows[k], rows[t]
                        ins = dve.tensor_tensor(yt_hl[1][0:f, k, 0:r], ps[2 + t % 2][0:f, 1, k * P:k * P + r],
                                                yt_hl[0][0:f, k, 0:r].bitcast(F32), ALU.subtract)
                    ins.then_inc(s_ylo, 1)
                t = s - 2
                if 0 <= t < T:
                    r = rows[t]
                    dve.wait_ge(s_o, t + 1)
                    dve.wait_ge(s_xh, t + 1)
                    dve.tensor_tensor(y_acc[0:r, t, :], y_acc[0:r, t, :],
                                      ps[0][0:r, :, :].rearrange("p a n -> p (a n)"), ALU.add).then_inc(s_x2, 1)
                    stats(t, T + t, s_x2, t + 1)
                t = s - 4
                if 0 <= t < T:
                    split_rows_lo(t, T + t)

            def split_lo(pair, u):
                raw_v, hi_v, lo_v = unit_views(u)
                dve.wait_ge(s_hi, unit(pair, u) + 1)
                dve.tensor_tensor(lo_v, raw_v, hi_v.bitcast(F32), ALU.subtract).then_inc(s_lo, 1)

            dve.wait_ge(s_g, 1)
            for t in range(T):
                r = rows[t]
                step(dve.tensor_tensor(gate[0:r, t, :], ps[2][0:r, 0, t * NE:(t + 1) * NE], rb_row[0:r, :], ALU.add))
            for t in range(T):
                step(dve.max(top[:, t, :], gate[:, t, :]))
                step(dve.max_index(top_i[:, t, :], top[:, t, :], gate[:, t, :]))
            step(dve.tensor_tensor(gd[:, :], top[:, :, 1], top[:, :, 0], ALU.subtract))
            dve.tensor_copy(top_f[:, :, :], top_i[:, :, 0:2]).then_inc(s_gd, 1)
            split_lo(0, 0)
            split_lo(0, 1)
            dve.wait_ge(s_ge, 1)
            step(dve.tensor_scalar(gs[:, :], ge[:, :], 1.0, None, ALU.add))
            step(dve.reciprocal(pr[:, 0, :], gs[:, :]))
            step(dve.tensor_tensor(pr[:, 1, :], pr[:, 0, :], ge[:, :], ALU.mult))

            def over(ap, shape):
                return ap.to_broadcast(shape)
            ei = e_idx[:, :].rearrange("p (a e) -> p a e", a=1).to_broadcast([P, T, NE])
            for j in range(2):
                tf = top_f[:, :, j:j + 1].to_broadcast([P, T, NE])
                pj = pr[:, j, :].rearrange("p (t a) -> p t a", a=1).to_broadcast([P, T, NE])
                step(dve.tensor_tensor(hot[:, j], tf, ei, ALU.is_equal))
                step(dve.tensor_tensor(hot[:, j], hot[:, j], pj, ALU.mult))
            step(dve.memset(w_sb[:, :, NE:NX], 1.0 / NS))
            dve.tensor_tensor(w_sb[:, :, 0:NE], hot[:, 0], hot[:, 1], ALU.add).then_inc(s_w, 1)

            def hidden_scale(pair, q, e):
                hq = 2 * KH * pair + q
                dve.wait_ge(f_g, hq + 1)
                if e is None:
                    dve.tensor_scalar(g_sb[q % 2], g_sb[q % 2], 1.0 / NS, None, ALU.mult).then_inc(f_m, 1)
                else:
                    row = wb[:, bass.ds(e + q // KH, 1), :].rearrange("p a n -> p (a n)") \
                        if not isinstance(e, int) else wb[:, e + q // KH, :]
                    dve.tensor_tensor(g_sb[q % 2], g_sb[q % 2], row, ALU.mult).then_inc(f_m, 1)

            def hidden_lo(pair, q):
                hq = 2 * KH * pair + q
                dve.wait_ge(f_hi, hq + 1)
                dve.tensor_tensor(ht_hl[1][:, q, :], g_sb[q % 2], ht_hl[0][:, q, :].bitcast(F32),
                                  ALU.subtract).then_inc(f_lo, 1)

            def add_block(pair, b):
                t, h = block_of(b)
                n = 2 * T * pair + b
                dve.wait_ge(f_y, n + 1)
                dve.wait_ge(f_acc, n - 2 * T + 1) if not isinstance(pair, int) or pair > 0 else None
                dve.tensor_tensor(y_acc[0:rows[t], t, h * DH:(h + 1) * DH], y_acc[0:rows[t], t, h * DH:(h + 1) * DH],
                                  ps[2 + b % 4 // 2][0:rows[t], b % 2, :], ALU.add).then_inc(f_acc, 1)

            def pair_dve(pair, e, last):
                split_lo(pair, 2)
                for q in range(2):
                    hidden_scale(pair, q, e)
                for q in range(2):
                    hidden_lo(pair, q)
                split_lo(pair, 3)
                for q in range(2, 4):
                    hidden_scale(pair, q, e)
                for q in range(2, 4):
                    hidden_lo(pair, q)
                if e is None:
                    dve.wait_ge(s_wt, 1)
                    dve.tensor_copy(w_t[:, 0:N], ps[2][0:NX, :, :].rearrange("p a n -> p (a n)")[:, 0:N]) \
                       .then_inc(s_wts, 1)
                for b in range(2 * T):
                    add_block(pair, b)
                    if not last and b in (1, 4):
                        split_lo(pair + 1, b // 3)

            step(dve.memset(wb[:, :, N:NP], 0.0))
            pair_dve(0, None, False)
            dve.wait_ge(s_wbs, NE)
            with dve.Fori(0, NRP - 1) as i:
                pair_dve(i + 1, 2 * i, False)
            pair_dve(NRP, 2 * NRP - 2, True)

        @block.tensor
        def _(pe):
            def hilo(out_ap, parts, start=True, stop=True):
                n = 3 * len(parts)
                k = 0
                for (lh, ll), (rh, rl) in parts:
                    for a, b in ((lh, rh), (lh, rl), (ll, rh)):
                        ins = pe.matmul(out_ap, a, b, start=start and k == 0, stop=stop and k == n - 1)
                        k += 1
                return ins

            for primed in (*s_used, s_ct):
                pe.sem_inc(primed, 1)
            pe.wait_ge(s_const, N_CONST)
            pe.wait_ge(s_kf, 1)
            for n, v in enumerate((key_f, src_f)):
                for j in range(2):
                    c = (2 * n + j) * G
                    pe.transpose(ps[2][0:CE, 0, c:c + G], v[:, j * CE:(j + 1) * CE], ident[0:G, 0:G])
            for n in range(2):
                ins = pe.matmul(ps[3][0:NW, 0, n * G:(n + 1) * G], kmm_b[:, n, :], ident[0:G, 0:G],
                                start=True, stop=True)
            ins.then_inc(s_kt, 1)

            def rows_t(source, ready, t, n):
                pe.wait_ge(ready, t + 1)
                if n >= 2:
                    pe.wait_ge(s_xlo, n - 1 if n < T else n)
                for k in range(KD):
                    ins = pe.transpose(ps_rows(n)[:, k, 0:rows[t]], source[t % 2][0:rows[t], k * P:(k + 1) * P],
                                       ident[0:rows[t], 0:rows[t]])
                ins.then_inc(s_xr, 1)

            for t in range(T):
                rows_t(xn, s_n, t, t)
            pe.wait_ge(s_rng, 1)
            pe.matmul(ps[3][0:1, 1, 0:NW], rng[:, 2:3], ident[0:NW, 0:NW], start=True, stop=True)
            pe.matmul(ps[3][0:1, 1, NW:2 * NW], rng[:, 3:4], ident[0:NW, 0:NW], start=True, stop=True)
            pe.matmul(ps[3][0:1, 1, 2 * NW:3 * NW], rng[:, 3:4], tri[:, :], start=True, stop=True).then_inc(s_rt, 1)
            pe.wait_ge(s_win, 1)
            pe.wait_ge(s_xlo, T)

            with pe.Fori(0, NW // 2) as i:
                for u in range(2):
                    first, number, before = window_regs(pe, win, NW, i, u, G)
                    pe.wait_ge(s_cs, 2 * i + 1)
                    for a in range(2):
                        pe.matmul(ps[u][0:WK, a, 0:NSL], zeros[:, 0:WK], zeros[:, WK:WK + NSL],
                                  start=True, stop=False)
                    with pe.Fori(0, number) as j:
                        for c in range(2):
                            pe.wait_ge(s_hot[c], before + j + 1)
                            for a in range(2):
                                ins = pe.matmul(ps[u][0:WK, a, 0:NSL], key_hot[c],
                                                src_hot[c][:, a * NSL:(a + 1) * NSL], start=False, stop=False)
                            ins.then_inc(s_used[c], 1)
                    for a in range(2):
                        ins = pe.matmul(ps[u][0:WK, a, 0:NSL], zeros[:, 0:WK], zeros[:, WK:WK + NSL],
                                        start=False, stop=True)
                    ins.then_inc(s_c, 1)
                for u in range(2):
                    pe.wait_ge(s_dg, 2 * i + u + 1)
                    pe.wait_ge(s_at, 2 * i + 1)
                    for s in range(T):
                        ins = pe.matmul(ps[2 + u][0:rows[s], s // 4, (s % 4) * WK:(s % 4 + 1) * WK],
                                        cnt_sb[u][:, s * P:s * P + rows[s]], diag, start=True, stop=True)
                    ins.then_inc(s_ct, 1)

            pe.wait_ge(s_lo, R)
            pe.wait_ge(s_cs, NW + 1)
            for t in range(T):
                if t >= 2:
                    pe.wait_ge(s_hs, t - 1)
                cols = slice(t * P, t * P + rows[t])
                for r in range(R):
                    ins = hilo(ps[t % 2][0:rows[t], r, 0:F],
                               [((xt[:, 0, k, cols], xt[:, 1, k, cols]), (rel_hl[0][:, r, k], rel_hl[1][:, r, k]))
                                for k in range(KD)])
                ins.then_inc(s_h, 1)

            def aggregate(t):
                pe.wait_ge(s_ylo, t - 1) if t >= 2 else None
                cols = slice(t * P, t * P + rows[t])
                o = ps[2 + t % 2][0:rows[t], 0, 0:F]
                hilo(o, [((xt[:, 0, k, cols], xt[:, 1, k, cols]), (root_hl[0][:, k], root_hl[1][:, k]))
                         for k in range(KD)], stop=False)
                for r in range(R):
                    for s in range(T):
                        ins = pe.matmul(o, a_t[0:rows[s], s, r, cols], h_rel[0:rows[s], s, r, :],
                                        start=False, stop=(r == R - 1 and s == T - 1))
                ins.then_inc(s_agg, 1)

            pe.wait_ge(s_lo, NG)
            pe.wait_ge(s_at, NW + 1)
            pe.wait_ge(s_hs, T)
            for s in range(T + 4):
                if s < T:
                    aggregate(s)
                t = s - 1
                if 0 <= t < T:
                    pe.wait_ge(s_y, t + 1)
                    for k in range(KF):
                        ins = pe.transpose(ps[2 + t % 2][0:frows[k], 1, k * P:k * P + rows[t]],
                                           z_sb[0:rows[t], k * FK:k * FK + frows[k]], ident[0:rows[t], 0:rows[t]])
                    ins.then_inc(s_yt, 1)
                t = s - 2
                if 0 <= t < T:
                    pe.wait_ge(s_ylo, t + 1)
                    if t >= 1:
                        pe.wait_ge(s_x2, t)
                    for h in range(2):
                        ins = hilo(ps[0][0:rows[t], h, :],
                                   [((yt_hl[0][0:frows[k], k, 0:rows[t]], yt_hl[1][0:frows[k], k, 0:rows[t]]),
                                     (wo_hl[0][0:frows[k], k, h * DH:(h + 1) * DH],
                                      wo_hl[1][0:frows[k], k, h * DH:(h + 1) * DH])) for k in range(KF)])
                    ins.then_inc(s_o, 1)
                t = s - 4
                if 0 <= t < T:
                    rows_t(x3, s_x3, t, T + t)

            pe.wait_ge(s_xlo, 2 * T)
            pe.wait_ge(s_rw, 2)
            for t in range(T):
                cols = slice(t * P, t * P + rows[t])
                ins = hilo(ps[2][0:rows[t], 0, t * NE:(t + 1) * NE],
                           [((xt[:, 0, k, cols], xt[:, 1, k, cols]), (rw_hl[0][:, k], rw_hl[1][:, k]))
                            for k in range(KD)])
            ins.then_inc(s_g, 1)
            pe.transpose(ps[2][:, 1, 0:NX * KH], b1_rows[:, :], ident[0:NX * KH, 0:NX * KH]).then_inc(s_bt, 1)

            def up_expert(pair, e):
                pe.wait_ge(s_lo, unit(pair, e) + 1)
                for m in range(KH):
                    q = KH * e + m
                    hq = 2 * KH * pair + q
                    if not isinstance(pair, int) or hq >= 2:
                        pe.wait_ge(f_g, hq - 1)
                    for a in range(2):
                        ins = hilo(ps[q % 2][:, a, 0:NL],
                                   [((w1_hl[0][:, e, k, m * P:(m + 1) * P], w1_hl[1][:, e, k, m * P:(m + 1) * P]),
                                     (xt[:, 0, k, a * NL:(a + 1) * NL], xt[:, 1, k, a * NL:(a + 1) * NL]))
                                    for k in range(KD)])
                    ins.then_inc(f_h, 1)

            def down_pair(pair, bias):
                def part(b, experts, start, stop):
                    t, h = block_of(b)
                    cols = slice(t * P, t * P + rows[t])
                    return hilo(ps[2 + b % 4 // 2][0:rows[t], b % 2, :],
                                [((ht_hl[0][:, KH * e + m, cols], ht_hl[1][:, KH * e + m, cols]),
                                  (w2_hl[0][:, e, m, h * DH:(h + 1) * DH], w2_hl[1][:, e, m, h * DH:(h + 1) * DH]))
                                 for e in experts for m in range(KH)], start=start, stop=stop)

                def opened(b):
                    n = 2 * T * pair + b
                    if not isinstance(n, int) or n >= 4:
                        pe.wait_ge(f_acc, n - 1 if b < 2 else n - 3)
                    if bias:
                        t, h = block_of(b)
                        pe.matmul(ps[2 + b % 4 // 2][0:rows[t], b % 2, :], w_t[:, t * P:t * P + rows[t]],
                                  b2_sb[:, h * DH:(h + 1) * DH], start=True, stop=False)
                    return not bias

                pe.wait_ge(s_lo, unit(pair, 2) + 1)
                pe.wait_ge(f_lo, 2 * KH * pair + KH)
                for b in range(4):
                    part(b, (0,), opened(b), False)
                pe.wait_ge(s_lo, unit(pair, 3) + 1)
                pe.wait_ge(f_lo, 2 * KH * pair + 2 * KH)
                for b in range(2 * T):
                    if b < 4:
                        ins = part(b, (1,), False, True)
                    else:
                        ins = part(b, (0, 1), opened(b), True)
                    ins.then_inc(f_y, 1)

            def pair_pe(pair):
                up_expert(pair, 0)
                up_expert(pair, 1)
                down_pair(pair, False)

            up_expert(0, 0)
            up_expert(0, 1)
            pe.wait_ge(s_w, 1)
            pe.wait_ge(s_rw, 3)
            for t in range(T):
                ins = pe.transpose(ps[2][:, :, :].rearrange("p a n -> p (a n)")[0:NX, t * P:t * P + rows[t]],
                                   w_sb[0:rows[t], t, :], ident[0:rows[t], 0:rows[t]])
            ins.then_inc(s_wt, 1)
            pe.wait_ge(s_wts, 1)
            pe.wait_ge(s_b2, 32)
            down_pair(0, True)
            for e in range(NE):
                if e < 2:
                    pe.wait_ge(f_acc, 2 * T)
                else:
                    pe.wait_ge(s_wbs, e - 1)
                for t in range(T):
                    ins = pe.matmul(ps[2 + e % 2][:, :, :].rearrange("p a n -> p (a n)")[:, t * P:t * P + rows[t]],
                                    w_sb[0:rows[t], t, e:e + 1].to_broadcast([rows[t], P]),
                                    ident[0:rows[t], 0:rows[t]], start=True, stop=True)
                ins.then_inc(s_wb, 1)
            pe.wait_ge(s_wbs, NE)
            with pe.Fori(0, NRP) as i:
                pair_pe(i + 1)
    return nc


INS = ["x", "src", "dst", "edge_type_2", "L0_gnn_ln_weight", "L0_gnn_W_rel", "L0_gnn_W_root", "L0_gnn_conv_bias",
       "L0_gnn_wo_weight", "L0_ffn_rW", "L0_ffn_rb", "L0_ffn_W1", "L0_ffn_b1", "L0_ffn_W2", "L0_ffn_b2",
       "L0_ffn_sW1", "L0_ffn_sb1", "L0_ffn_sW2", "L0_ffn_sb2"]


def kernel(**inputs):
    import numpy as np
    import concourse.bacc as bacc
    from concourse.bass_utils import run_bass_kernel_spmd

    nc = bacc.Bacc("TRN2", target_bir_lowering=False, num_devices=1)
    arrays, args = {}, []
    for name in INS:
        a = np.ascontiguousarray(inputs[name])
        arrays[f"in_{name}"] = a
        args.append(nc.dram_tensor(f"in_{name}", a.shape, mybir.dt.from_np(a.dtype), kind="ExternalInput").ap())
    out = nc.dram_tensor("out", inputs["x"].shape, F32, kind="ExternalOutput").ap()
    program(nc, *args, out)
    return run_bass_kernel_spmd(nc, [arrays], core_ids=[0]).results[0]["out"]
```

```python
import concourse.bass as bass
from concourse import mybir
from contextlib import ExitStack

F32 = mybir.dt.float32
F32R = mybir.dt.float32r
F16 = mybir.dt.float16
I32 = mybir.dt.int32
U32 = mybir.dt.uint32
ALU = mybir.AluOpType
ACT = mybir.ActivationFunctionType
AX = mybir.AxisListType


class Tally:

    def __init__(self, sem):
        self.sem, self.n, self.off = sem, 0, 0

    def mark(self, ins):
        ins.then_inc(self.sem, 1)
        self.n += 1
        return self.n + self.off

    def now(self):
        return self.n + self.off


def window_regs(eng, win, NW, at, G):
    first = eng.value_load(win[0:1, bass.ds(at, 1)], min_val=0, max_val=G - 1)
    number = eng.value_load(win[0:1, bass.ds(NW + at, 1)], min_val=1, max_val=G)
    before = eng.value_load(win[0:1, bass.ds(2 * NW + at, 1)], min_val=0, max_val=NW * G)
    return first, number, before


def program(nc, x, src, dst, rel, ln_w, w_rel, w_root, conv_b, wo, rw, rb, w1, b1, w2, b2, sw1, sb1, sw2, sb2, out):
    N, D = x.shape
    E = src.shape[0]
    R, _, F = w_rel.shape
    NE, _, HID = w1.shape
    NS = sw1.shape[0]
    NX = NE + NS
    P = 128
    T = -(-N // P)
    rows = [min(P, N - t * P) for t in range(T)]
    KD = D // P
    KH = HID // P
    NP = 628
    NL = NP // 2
    CE = 125
    CG = 4
    EG = CG * CE
    G = E // EG
    assert G * EG == E
    KEYS = R * N
    WK = 126
    WD = WK // R
    NW = -(-KEYS // WK)
    ND = NW * WD
    assert NW * WK <= 2048
    NSRC = T * P
    FK = 96
    KF = -(-F // FK)
    frows = [min(FK, F - k * FK) for k in range(KF)]
    DH = D // 2

    ctx = ExitStack()
    with ctx:
        def sb(name, shape, dt=F32):
            return ctx.enter_context(nc.sbuf_tensor(name, shape, dt))

        def sem(name):
            return ctx.enter_context(nc.semaphore(name))

        xt = sb("xt", [P, 2, KD, NP], F32R)
        y_acc = sb("y_acc", [P, T, D])
        ident = sb("ident", [P, P])
        W_REL, W_ROOT, W_O = R * KD * F, KD * F, KF * D
        UNIT = KD * HID
        assert UNIT == KH * D
        arena_r = sb("arena_r", [P, 8 * UNIT + 4 * KH * NP], F32R)
        at = 0

        def cut(n):
            nonlocal at
            at += n
            return arena_r[:, at - n:at]
        rel_hl = [cut(W_REL).rearrange("p (r k f) -> p r k f", r=R, k=KD) for _ in range(2)]
        root_hl = [cut(W_ROOT).rearrange("p (k f) -> p k f", k=KD) for _ in range(2)]
        wo_hl = [cut(W_O).rearrange("p (k n) -> p k n", k=KF) for _ in range(2)]
        yt_hl = [cut(KF * P).rearrange("p (k n) -> p k n", k=KF) for _ in range(2)]
        assert at <= arena_r.shape[1]
        at = 0
        w1_hl = [cut(2 * UNIT).rearrange("p (e k n) -> p e k n", e=2, k=KD) for _ in range(2)]
        w2_hl = [cut(2 * UNIT).rearrange("p (e k n) -> p e k n", e=2, k=KH) for _ in range(2)]
        ht_hl = [cut(2 * KH * NP).rearrange("p (q n) -> p q n", q=2 * KH) for _ in range(2)]
        big = sb("big", [P, max(T * R * ND, NX * NP)])
        h0 = [big[:, i * D:(i + 1) * D] for i in range(2)]
        xn = [big[:, (2 + i) * D:(3 + i) * D] for i in range(2)]
        dst_i, rel_i = (big[0:G, 5 * D + i * EG:5 * D + (i + 1) * EG].bitcast(I32) for i in range(2))
        assert 5 * D + 2 * EG <= big.shape[1]
        lnw_row = big[:, 4 * D:5 * D]
        a_t = big[:, 0:T * R * ND].rearrange("p (s r d) -> p s r d", s=T, r=R)
        wb = big[:, 0:NX * NP].rearrange("p (e n) -> p e n", e=NX)
        SLOT = KD * F
        raw = sb("raw", [P, 2 * SLOT])
        slot = [raw[:, i * SLOT:(i + 1) * SLOT] for i in range(2)]
        HF = F + 2
        h_at = {0: SLOT - 2 * R * HF, 1: SLOT - R * HF, 2: 0, 3: SLOT, 4: SLOT + R * HF}
        assert T == len(h_at) and 3 * R * HF <= SLOT and SLOT - 2 * R * HF >= D
        h_rel = [raw[:, h_at[t]:h_at[t] + R * HF].rearrange("p (r f) -> p r f", r=R) for t in range(T)]
        work = sb("work", [P, 2 * D])
        src_i = work[0:G, 0:EG].bitcast(I32)
        key_f = work[0:G, EG:2 * EG]
        src_f = work[0:G, 2 * EG:3 * EG]
        hot_at = CG * WK // 2
        key_hot = work[0:CE, 0:hot_at].bitcast(F16).rearrange("p (c k) -> p c k", c=CG)
        src_hot = [work[0:CE, hot_at + c * NSRC // 2:hot_at + (c + 1) * NSRC // 2].bitcast(F16) for c in range(CG)]
        dif_at = hot_at + CG * NSRC // 2
        key_dif = work[0:CE, dif_at:dif_at + CG * WK // 2].bitcast(F16).rearrange("p (c k) -> p c k", c=CG)
        assert dif_at + CG * WK // 2 <= 2 * D
        x3 = [work[:, i * D:(i + 1) * D] for i in range(2)]
        g_sb = [work[:, i * NP:(i + 1) * NP] for i in range(2)]
        late = sb("late", [P, D])
        iota = late[:, 0:NW * WK // 2].bitcast(F16)
        b2_sb = late[0:NX, :]
        mid = sb("mid", [P, 3 * F])
        z_sb, m_sb, e_sb = (mid[:, i * F:(i + 1) * F] for i in range(3))
        w_t = mid[0:NX, 0:NP]
        key_t = mid[0:CE, 0:CG * G].rearrange("p (j g) -> p j g", j=CG)
        src_t = mid[0:CE, CG * G:2 * CG * G].rearrange("p (j g) -> p j g", j=CG)
        bias_row = sb("bias_row", [P, F])
        rw_sb = sb("rw_sb", [P, KD, NE])
        rw_hl = sb("rw_hl", [P, KD, 2, NE], F32R)
        ident_r = sb("ident_r", [P, P], F32R)
        w_hl = sb("w_hl", [P, 2, T, NX], F32R)
        rb_row = sb("rb_row", [P, NE])
        b1_rows = sb("b1_rows", [NX * KH, P])
        b1_t = sb("b1_t", [P, NX * KH])
        zeros = sb("zeros", [1, 4 * WK], F16)
        st = sb("st", [P, 2, 6])
        mv = sb("mv", [P, T, 2])
        rstd = sb("rstd", [P, T])
        minus_half = sb("minus_half", [P, 1])
        rstd_1 = sb("rstd_1", [P, T])
        nmr = sb("nmr", [P, T])
        sumsq = sb("sumsq", [P, T])
        rms = sb("rms", [P, T])
        kmm = sb("kmm", [G, 2])
        kmm_b = sb("kmm_b", [G, 2, NW])
        first_key = sb("first_key", [NW, 1])
        last_key = sb("last_key", [NW, 1])
        down, up, act_a, act_b = (late[0:NW, D - (i + 1) * G:D - i * G] for i in range(4))
        rng = sb("rng", [NW, 4])
        tri = sb("tri", [NW, NW])
        win = sb("win", [1, 3 * NW], I32)
        cnt = sb("cnt", [P, R])
        inv = sb("inv", [P, R])
        gate = sb("gate", [P, T, NE])
        top = sb("top", [P, T, 8])
        top_i = sb("top_i", [P, T, 8], U32)
        top_f = sb("top_f", [P, T, 2])
        gd = sb("gd", [P, T])
        ge = sb("ge", [P, T])
        gs = sb("gs", [P, T])
        pr = sb("pr", [P, 2, T])
        hot = sb("hot", [P, 2, T, NE])
        e_idx = sb("e_idx", [P, NE])
        w_sb = sb("w_sb", [P, T, NX])

        ps = [ctx.enter_context(nc.psum_tensor(f"ps{i}", [P, 2, 512], F32)) for i in range(4)]

        def ps_rows(n):
            return ps[n % 2 if n < T else 1][:, :, :].rearrange("p a (b c) -> p (a b) c", c=P)

        s_x = [sem(f"s_xin{t}") for t in range(T)]
        s_edge = sem("s_edge")
        s_lnw = sem("s_lnw")
        s_small = sem("s_small")
        s_b1 = sem("s_b1")
        s_b2 = sem("s_b2")
        s_raw = [sem(f"s_raw{i}") for i in range(2)]
        s_const = sem("s_const")
        s_hi = sem("s_hi")
        s_lo = sem("s_lo")
        s_v = sem("s_v")
        s_a = sem("s_a")
        s_kf = sem("s_kf")
        s_kt = sem("s_kt")
        s_rng = sem("s_rng")
        s_rt = sem("s_rt")
        s_win = sem("s_win")
        s_ln = sem("s_ln")
        s_p = sem("s_p")
        s_mv = sem("s_mv")
        s_rms = sem("s_rms")
        s_h0 = sem("s_h0")
        s_xh = sem("s_xh")
        s_n = sem("s_n")
        s_xr = sem("s_xr")
        s_xhi = sem("s_xhi")
        s_xlo = sem("s_xlo")
        s_hot = [sem(f"s_hot{u}") for u in range(2)]
        s_used = [sem(f"s_used{u}") for u in range(2)]
        s_dif = [sem(f"s_dif{u}") for u in range(2)]
        s_eq = [sem(f"s_eq{u}") for u in range(2)]
        s_c = sem("s_c")
        s_ones = sem("s_ones")
        s_at = sem("s_at")
        s_h = sem("s_h")
        s_hs = sem("s_hs")
        s_agg = sem("s_agg")
        s_m = sem("s_m")
        s_e = sem("s_e")
        s_y = sem("s_y")
        s_yt = sem("s_yt")
        s_yhi = sem("s_yhi")
        s_ylo = sem("s_ylo")
        s_o = sem("s_o")
        s_x2 = sem("s_xtwo")
        s_x3 = sem("s_xthree")
        s_rw = sem("s_rw")
        s_b1t = sem("s_b1t")
        s_bt = sem("s_bt")
        s_g = sem("s_g")
        s_wr = sem("s_wr")
        s_gd = sem("s_gd")
        s_ge = sem("s_ge")
        s_w = sem("s_w")
        s_wt = sem("s_wt")
        s_wts = sem("s_wts")
        s_wb = sem("s_wb")
        s_wbs = sem("s_wbs")
        f_h = sem("f_h")
        f_g = sem("f_g")
        f_m = sem("f_m")
        f_hi = sem("f_hi")
        f_lo = sem("f_lo")
        f_y = sem("f_y")
        f_acc = sem("f_acc")
        s_out = sem("s_out")

        NG = 5
        NPAIR = NX // 2
        NRP = NE // 2

        def unit(pair, u):
            return NG + 4 * pair + u

        def w_slot(u):
            return (NG + u) % 2

        block = ctx.enter_context(nc.Block())

        @block.sync
        def _(sp):
            def load_x(t):
                sp.dma_start(y_acc[0:rows[t], t, :], x[t * P:t * P + rows[t], :]).then_inc(s_x[t], 16)

            def raw_free(n):
                if not isinstance(n, int) or n >= 2:
                    sp.wait_ge(s_lo, n - 1)

            load_x(0)
            load_x(1)
            sp.dma_start(lnw_row, ln_w.rearrange("(a n) -> a n", a=1).to_broadcast([P, D])).then_inc(s_lnw, 16)
            for t in range(2, T):
                load_x(t)
            for n in range(R):
                sp.dma_start(slot[n].rearrange("p (k f) -> p k f", k=KD),
                             w_rel[n].rearrange("(k p) f -> p k f", p=P)).then_inc(s_raw[n], 16)
            sp.dma_start(bias_row[:, :], conv_b.rearrange("(a n) -> a n", a=1).to_broadcast([P, F])).then_inc(s_lnw, 16)
            raw_free(2)
            sp.dma_start(slot[0].rearrange("p (k f) -> p k f", k=KD),
                         w_root.rearrange("(k p) f -> p k f", p=P)).then_inc(s_raw[0], 16)
            raw_free(3)
            sp.dma_start(slot[1][0:FK, 0:2 * D].rearrange("p (k n) -> p k n", k=2),
                         wo[0:2 * FK, :].rearrange("(k p) n -> p k n", p=FK)).then_inc(s_raw[1], 16)
            raw_free(4)
            sp.dma_start(slot[0][0:frows[2], 0:D], wo[2 * FK:F, :]).then_inc(s_raw[0], 16)
            sp.dma_start(rw_sb[:, :, :], rw.rearrange("(k p) e -> p k e", p=P)).then_inc(s_small, 16)
            sp.dma_start(rb_row[:, :], rb.rearrange("(a n) -> a n", a=1).to_broadcast([P, NE])).then_inc(s_small, 16)
            sp.wait_ge(s_c, NW)
            sp.dma_start(b2_sb[0:NE, :], b2).then_inc(s_b2, 16)
            sp.dma_start(b2_sb[NE:NX, :], sb2).then_inc(s_b2, 16)
            sp.wait_ge(s_agg, T)

            def load_pair(w1s, w2s, pair):
                for u in range(4):
                    raw_free(unit(pair, u))
                    s = w_slot(u)
                    if u < 2:
                        sp.dma_start(slot[s][:, 0:UNIT].rearrange("p (k n) -> p k n", k=KD),
                                     w1s(u)).then_inc(s_raw[s], 16)
                    else:
                        sp.dma_start(slot[s][:, 0:UNIT].rearrange("p (k n) -> p k n", k=KH),
                                     w2s(u - 2)).then_inc(s_raw[s], 16)

            load_pair(lambda e: sw1[e].rearrange("(k p) n -> p k n", p=P),
                      lambda e: sw2[e].rearrange("(k p) n -> p k n", p=P), 0)
            w1v = w1.rearrange("e (k p) n -> e p k n", p=P)
            w2v = w2.rearrange("e (k p) n -> e p k n", p=P)
            with sp.Fori(0, NRP) as i:
                load_pair(lambda e: w1v[bass.ds(2 * i + e, 1)].rearrange("e p k n -> (e p) k n"),
                          lambda e: w2v[bass.ds(2 * i + e, 1)].rearrange("e p k n -> (e p) k n"), i + 1)
            for t in range(T):
                sp.wait_ge(f_acc, 2 * T * (NPAIR - 1) + 2 * t + 2)
                sp.dma_start(out[t * P:t * P + rows[t], :], y_acc[0:rows[t], t, :]).then_inc(s_out, 16)
            sp.wait_ge(s_out, 16 * T)

        N_CONST = 14

        def kf2(v, n):
            return v.rearrange("p (k n) -> p k n", k=n)
        gnn_units = [(kf2(slot[0], KD), rel_hl[0][:, 0], rel_hl[1][:, 0]),
                     (kf2(slot[1], KD), rel_hl[0][:, 1], rel_hl[1][:, 1]),
                     (kf2(slot[0], KD), root_hl[0], root_hl[1]),
                     (kf2(slot[1][0:FK, 0:2 * D], 2), wo_hl[0][0:FK, 0:2], wo_hl[1][0:FK, 0:2]),
                     (slot[0][0:frows[2], 0:D], wo_hl[0][0:frows[2], 2], wo_hl[1][0:frows[2], 2])]

        def group_of(first, j):
            return nc.s_assert_within(
                first + j, 0, G - 1, skip_runtime_bounds_check_because=
                "first + number is the end of the window's range, at most G whatever the keys are")

        @block.gpsimd
        def _(pool):
            k = Tally(s_const)
            k.mark(pool.memset(ident[:, :], 0.0))
            k.mark(pool.memset(tri[:, :], 0.0))
            k.mark(pool.iota(iota, [[1, NW * WK]], base=0, channel_multiplier=0,
                             allow_small_or_imprecise_dtypes=True))
            k.mark(pool.iota(first_key[:, :], [[0, 1]], base=0, channel_multiplier=WK,
                             allow_small_or_imprecise_dtypes=True))
            k.mark(pool.iota(last_key[:, :], [[0, 1]], base=WK - 1, channel_multiplier=WK,
                             allow_small_or_imprecise_dtypes=True))
            k.mark(pool.iota(down, [[-1, G]], base=G, channel_multiplier=0,
                             allow_small_or_imprecise_dtypes=True))
            k.mark(pool.iota(up, [[1, G]], base=1, channel_multiplier=0,
                             allow_small_or_imprecise_dtypes=True))
            k.mark(pool.iota(e_idx[:, :], [[1, NE]], base=0, channel_multiplier=0,
                             allow_small_or_imprecise_dtypes=True))
            k.mark(pool.memset(zeros[:, :], 0.0))
            k.mark(pool.memset(xt[:, :, :, N:NP].bitcast(F32), 0.0))
            k.mark(pool.memset(gate[:, :, :], 0.0))
            k.mark(pool.memset(minus_half[:, :], -0.5))
            pool.wait_ge(s_const, 2)
            k.mark(pool.affine_select(out=ident[:, :], in_=ident[:, :], compare_op=ALU.not_equal, fill=1.0,
                                      base=0, pattern=[[-1, P]], channel_multiplier=1))
            k.mark(pool.affine_select(out=tri[:, :], in_=tri[:, :], compare_op=ALU.is_ge, fill=1.0,
                                      base=0, pattern=[[-1, NW]], channel_multiplier=1))
            assert k.n == N_CONST
            own = Tally(s_p)
            pool.wait_ge(s_const, N_CONST)

            def row_scale(t, n):
                r = rows[t]
                pool.wait_ge(s_mv, n + 1)
                own.mark(pool.tensor_scalar(rstd[0:r, t:t + 1], mv[0:r, t, 1:2], 1.0, 1e-5, ALU.mult, ALU.add))
                pool.wait_ge(s_p, own.n)
                own.mark(pool.tensor_tensor(rstd[0:r, t:t + 1], rstd[0:r, t:t + 1], minus_half[0:r, :], ALU.pow))
                pool.wait_ge(s_p, own.n)
                if n < T:
                    own.mark(pool.tensor_scalar(rstd_1[0:r, t:t + 1], rstd[0:r, t:t + 1], 1.0, 1.0,
                                                ALU.mult, ALU.add))
                pool.tensor_scalar(nmr[0:r, t:t + 1], mv[0:r, t, 0:1], rstd[0:r, t:t + 1], -1.0,
                                   ALU.mult, ALU.mult).then_inc(s_ln, 1)

            def unit_lo(n):
                raw_v, hi_v, lo_v = gnn_units[n]
                pool.wait_ge(s_hi, n + 1)
                pool.tensor_tensor(lo_v, raw_v, hi_v.bitcast(F32), ALU.subtract).then_inc(s_lo, 1)

            row_scale(0, 0)
            for t in range(T):
                r = rows[t]
                if t + 1 < T:
                    row_scale(t + 1, t + 1)
                pool.wait_ge(s_h0, t + 1)
                own.mark(pool.tensor_scalar(rms[0:r, t:t + 1], sumsq[0:r, t:t + 1], 1.0 / D, 1e-6,
                                            ALU.mult, ALU.add))
                pool.wait_ge(s_p, own.n)
                pool.tensor_tensor(rms[0:r, t:t + 1], rms[0:r, t:t + 1], minus_half[0:r, :],
                                   ALU.pow).then_inc(s_rms, 1)
                if t in (1, 2):
                    unit_lo(t - 1)
            for n in range(2, NG):
                unit_lo(n)
            pool.wait_ge(s_lo, NG)
            for t in range(T):
                pool.memset(h_rel[t][:, :, F:HF], 1.0).then_inc(s_ones, 1)
            for t in range(T):
                r = rows[t]
                pool.tensor_scalar(y_acc[0:r, t, :], y_acc[0:r, t, :], rstd_1[0:r, t:t + 1], nmr[0:r, t:t + 1],
                                   ALU.mult, ALU.add).then_inc(s_xh, 1)
            for t in range(T):
                row_scale(t, T + t)

        def unit_views(u):
            raw_v = slot[w_slot(u)][:, 0:UNIT]
            if u < 2:
                return [kf2(raw_v, KD)] + [w[:, u] for w in w1_hl]
            return [kf2(raw_v, KH)] + [w[:, u - 2] for w in w2_hl]

        def h_bank(t):
            return 3 - t % 2

        def projected(w):
            return (2 + w // R, w % R) if w < R * (T - 2) else (None, None)

        def agg_views(t):
            bank = ps[2 + t % 2][0:rows[t]]
            cut = 512 - (F + 1)
            return bank[:, 0, 0:F], [[(0, bank[:, 1, 0:F + 1])],
                                     [(0, bank[:, 1, F + 1:512]), (cut, bank[:, 0, F:2 * F + 1 - cut])]]

        def wb_bank(e):
            return ps[(e + 1) % 2][:, :, :].rearrange("p a n -> p (a n)")

        def block_of(b):
            return b // 2, b % 2

        @block.scalar
        def _(act):
            v = Tally(s_a)
            for to, frm in ((dst_i, dst), (rel_i, rel), (src_i, src)):
                act.dma_start(to, frm.rearrange("(p e) -> p e", e=EG)).then_inc(s_edge, 16)
            act.dma_start(b1_rows[0:NE * KH, :], b1.rearrange("e (m p) -> (e m) p", p=P)).then_inc(s_b1, 16)
            act.dma_start(b1_rows[NE * KH:NX * KH, :], sb1.rearrange("e (m p) -> (e m) p", p=P)).then_inc(s_b1, 16)

            def split_rows(t, n):
                act.wait_ge(s_xr, n + 1)
                act.activation(xt[:, 0, :, t * P:t * P + rows[t]],
                               ps_rows(n)[:, :, 0:rows[t]], ACT.Copy).then_inc(s_xhi, 1)

            def unit_hi(n):
                raw_v, hi_v, _ = gnn_units[n]
                act.wait_ge(s_raw[n % 2], 16 * (n // 2 + 1))
                act.activation(hi_v, raw_v, ACT.Copy).then_inc(s_hi, 1)

            def h_out(t):
                act.wait_ge(s_h, t + 1)
                act.wait_ge(s_lo, 3 if t < 2 else NG)
                act.activation(h_rel[t][0:rows[t], :, 0:F], ps[h_bank(t)][0:rows[t], :, 0:F], ACT.Copy).then_inc(s_hs, 1)

            for s in range(T + 1):
                if s < T:
                    t, r = s, rows[s]
                    act.wait_ge(s_ln, t + 1)
                    if t >= 2:
                        act.wait_ge(s_xr, t - 1)
                        act.wait_ge(s_n, t - 1)
                    v.mark(act.activation(h0[t % 2][0:r, :], y_acc[0:r, t, :], ACT.Identity,
                                          bias=nmr[0:r, t:t + 1], scale=rstd[0:r, t:t + 1]))
                    act.wait_ge(s_a, v.n)
                    act.activation(xn[t % 2][0:r, :], h0[t % 2][0:r, :], ACT.Square,
                                   accum_out=sumsq[0:r, t:t + 1]).then_inc(s_h0, 1)
                if s >= 1:
                    split_rows(s - 1, s - 1)
                if s in (1, 2, 4):
                    unit_hi(min(s - 1, 2))
                if s == 2:
                    act.wait_ge(s_bt, 1)
                    act.activation(b1_t[:, :], ps[2][:, 1, 0:NX * KH], ACT.Copy).then_inc(s_b1t, 1)
            h_out(0)
            unit_hi(3)
            h_out(1)
            unit_hi(4)
            act.wait_ge(s_small, 32)
            act.activation(rw_hl[:, :, 0, :], rw_sb[:, :, :], ACT.Copy).then_inc(s_rw, 1)
            act.activation(ident_r[:, :], ident[:, :], ACT.Copy).then_inc(s_b1t, 1)
            act.wait_ge(s_n, T)
            act.wait_ge(s_win, 2)

            def window_difs(w):
                first, number, before = window_regs(act, win, NW, w, G)
                with act.Fori(0, number) as j:
                    group = group_of(first, j)
                    for h in range(2):
                        act.wait_ge(s_eq[h], before + j + 1)
                        for c in (2 * h, 2 * h + 1):
                            ins = act.activation(key_dif[:, c, :], iota[0:CE, w * WK:(w + 1) * WK], ACT.Identity,
                                                 bias=key_t[:, c, bass.ds(group, 1)], scale=-1.0)
                        ins.then_inc(s_dif[h], 1)

            def window_out(w):
                u = w % 2
                act.wait_ge(s_c, w + 1)
                act.activation(a_t[:, 0:T - 1, :, w * WD:(w + 1) * WD],
                               ps[u][:, 0, 0:(T - 1) * WK].rearrange("p (s d r) -> p s r d", s=T - 1, r=R),
                               ACT.Copy)
                act.activation(a_t[:, T - 1, :, w * WD:(w + 1) * WD],
                               ps[u][:, 1, 0:WK].rearrange("p (d r) -> p r d", r=R), ACT.Copy).then_inc(s_at, 1)
                t, r = projected(w)
                if t is not None and r == R - 1:
                    h_out(t)

            for w in range(NW):
                window_difs(w)
                if w >= 1:
                    window_out(w - 1)
            window_out(NW - 1)
            for s in range(T + 2):
                t = s - 2
                if 0 <= t < T:
                    r = rows[t]
                    act.wait_ge(s_ln, T + t + 1)
                    if t >= 2:
                        act.wait_ge(s_xr, T + t - 1)
                    act.activation(x3[t % 2][0:r, :], y_acc[0:r, t, :], ACT.Identity,
                                   bias=nmr[0:r, t:t + 1], scale=rstd[0:r, t:t + 1]).then_inc(s_x3, 1)
                t = s - 1
                if 0 <= t < T:
                    act.wait_ge(s_yt, t + 1)
                    if t >= 1:
                        act.wait_ge(s_o, t)
                    for k in range(KF):
                        ins = act.activation(yt_hl[0][0:frows[k], k, 0:rows[t]],
                                             ps[2 + t % 2][0:frows[k], 1, k * P:k * P + rows[t]], ACT.Copy)
                    ins.then_inc(s_yhi, 1)
                if s < T:
                    r = rows[s]
                    act.wait_ge(s_m, s + 1)
                    act.activation(e_sb[0:r, :], m_sb[0:r, :], ACT.Exp).then_inc(s_e, 1)
                t = s - 2
                if 0 <= t < T:
                    split_rows(t, T + t)

            def split_hi(pair, u):
                n = unit(pair, u)
                raw_v, hi_v, _ = unit_views(u)
                act.wait_ge(s_raw[w_slot(u)], 16 * ((n - w_slot(u)) // 2 + 1) if isinstance(pair, int)
                            else 16 * ((NG + u - w_slot(u)) // 2 + 1) + 32 * pair)
                if u < 2:
                    act.wait_ge(f_h, 2 * KH * pair)
                else:
                    act.wait_ge(f_y, 2 * T * pair)
                act.activation(hi_v, raw_v, ACT.Copy).then_inc(s_hi, 1)

            def hidden(pair, q, first_expert):
                hq = 2 * KH * pair + q
                act.wait_ge(f_h, hq + 1)
                act.wait_ge(f_lo, hq - 1) if not isinstance(hq, int) or hq >= 1 else None
                e = first_expert + q // KH
                col = b1_t[:, bass.ds(e * KH + q % KH, 1)] if not isinstance(e, int) else \
                    b1_t[:, e * KH + q % KH:e * KH + q % KH + 1]
                act.activation(g_sb[q % 2].rearrange("p (a n) -> p a n", a=2), ps[q % 2][:, :, 0:NL],
                               ACT.Gelu, bias=col).then_inc(f_g, 1)

            def hidden_hi(pair, q):
                hq = 2 * KH * pair + q
                act.wait_ge(f_m, hq + 1)
                act.wait_ge(f_y, 2 * T * pair)
                act.activation(ht_hl[0][:, q, :], g_sb[q % 2], ACT.Copy).then_inc(f_hi, 1)

            def pair_act(pair, first_expert, last):
                if isinstance(pair, int) and pair == 0:
                    split_hi(0, 0)
                    split_hi(0, 1)
                split_hi(pair, 2)
                hidden(pair, 0, first_expert)
                hidden(pair, 1, first_expert)
                hidden_hi(pair, 0)
                hidden_hi(pair, 1)
                split_hi(pair, 3)
                if isinstance(pair, int) and pair == 0:
                    act.wait_ge(s_gd, 1)
                    act.activation(ge[:, :], gd[:, :], ACT.Exp).then_inc(s_ge, 1)
                hidden(pair, 2, first_expert)
                hidden(pair, 3, first_expert)
                hidden_hi(pair, 2)
                hidden_hi(pair, 3)
                if not last:
                    if isinstance(pair, int) and pair == 0:
                        for e in range(2):
                            wb_copy(e)
                    split_hi(pair + 1, 0)
                    if isinstance(pair, int) and pair == 0:
                        for e in range(2, 6):
                            wb_copy(e)
                    split_hi(pair + 1, 1)

            def wb_copy(e):
                act.wait_ge(s_wb, e + 1)
                act.activation(wb[:, e, 0:N + 1], wb_bank(e)[:, 0:N + 1], ACT.Copy).then_inc(s_wbs, 1)

            pair_act(0, NE, False)
            for e in range(6, NE):
                wb_copy(e)
            with act.Fori(0, NRP - 1) as i:
                pair_act(i + 1, 2 * i, False)
            pair_act(NRP, 2 * NRP - 2, True)

        @block.vector
        def _(dve):
            v = Tally(s_v)

            def step(ins):
                v.mark(ins)
                dve.wait_ge(s_v, v.n)

            dve.wait_ge(s_const, N_CONST)
            dve.wait_ge(s_edge, 48)
            step(dve.scalar_tensor_tensor(key_f, dst_i, float(R), rel_i, ALU.mult, ALU.add))
            step(dve.tensor_copy(src_f, src_i))
            step(dve.tensor_reduce(kmm[:, 0:1], key_f, AX.X, ALU.min))
            step(dve.tensor_reduce(kmm[:, 1:2], key_f, AX.X, ALU.max))
            dve.tensor_copy(kmm_b[:, :, :], kmm[:, :].rearrange("p (a b) -> p a b", b=1)
                            .to_broadcast([G, 2, NW])).then_inc(s_kf, 1)

            def stats(t, n, ready, value):
                r = rows[t]
                dve.wait_ge(ready, value)
                for h in range(2):
                    v.mark(dve.bn_stats(st[0:r, h, :], y_acc[0:r, t, h * 512:(h + 1) * 512]))
                dve.wait_ge(s_v, v.n)
                dve.bn_aggr(mv[0:r, t, :], st[0:r, :, :]).then_inc(s_mv, 1)
                dve.wait_ge(s_mv, n + 1)

            def split_rows_lo(t, n):
                dve.wait_ge(s_xhi, n + 1)
                cols = slice(t * P, t * P + rows[t])
                dve.tensor_tensor(xt[:, 1, :, cols], ps_rows(n)[:, :, 0:rows[t]],
                                  xt[:, 0, :, cols].bitcast(F32), ALU.subtract).then_inc(s_xlo, 1)

            def ranges():
                dve.wait_ge(s_kt, 1)
                dve.tensor_copy(key_t, ps[2][0:CE, 0, 0:CG * G].rearrange("p (j g) -> p j g", j=CG))
                step(dve.tensor_copy(src_t, ps[2][0:CE, 0, CG * G:2 * CG * G].rearrange("p (j g) -> p j g", j=CG)))
                kmin, kmax = ps[3][0:NW, 0, 0:G], ps[3][0:NW, 0, G:2 * G]
                step(dve.tensor_scalar(act_a, kmax, first_key[:, :], None, ALU.is_ge))
                step(dve.scalar_tensor_tensor(act_a, kmin, last_key[:, :], act_a, ALU.is_le, ALU.mult))
                step(dve.tensor_tensor(act_b, act_a, down, ALU.mult))
                step(dve.tensor_tensor(act_a, act_a, up, ALU.mult))
                step(dve.tensor_reduce(rng[:, 0:1], act_b, AX.X, ALU.max))
                step(dve.tensor_reduce(rng[:, 1:2], act_a, AX.X, ALU.max))
                step(dve.tensor_scalar(rng[:, 2:3], rng[:, 0:1], -1.0, float(G), ALU.mult, ALU.add))
                step(dve.tensor_scalar(rng[:, 2:3], rng[:, 2:3], float(G - 1), None, ALU.min))
                step(dve.tensor_tensor(rng[:, 3:4], rng[:, 1:2], rng[:, 2:3], ALU.subtract))
                dve.tensor_scalar(rng[:, 3:4], rng[:, 3:4], 1.0, None, ALU.max).then_inc(s_rng, 1)

            for s in range(T + 2):
                if s < T:
                    stats(s, s, s_x[s], 16)
                t = s - 1
                if 0 <= t < T:
                    r = rows[t]
                    dve.wait_ge(s_rms, t + 1)
                    if t == 0:
                        dve.wait_ge(s_lnw, 32)
                    dve.scalar_tensor_tensor(xn[t % 2][0:r, :], h0[t % 2][0:r, :], rms[0:r, t:t + 1],
                                             lnw_row[0:r, :], ALU.mult, ALU.mult).then_inc(s_n, 1)
                t = s - 2
                if 0 <= t < T:
                    split_rows_lo(t, t)
                if s == 0:
                    ranges()
                if s == 2:
                    dve.wait_ge(s_rt, 1)
                    dve.tensor_copy(win[:, :], ps[3][0:1, 1, 0:3 * NW]).then_inc(s_win, 1)
            dve.wait_ge(s_win, 1)
            dve.sem_inc(s_win, 1)

            def window_hots(w):
                first, number, before = window_regs(dve, win, NW, w, G)
                with dve.Fori(0, number) as j:
                    group = group_of(first, j)
                    for h in range(2):
                        dve.wait_ge(s_used[h], before + j + 1)
                        cs = slice(2 * h, 2 * h + 2)
                        dve.wait_ge(s_dif[h], before + j + 1)
                        dve.tensor_scalar(key_hot[:, cs, :], key_dif[:, cs, :], 0.0, None,
                                          ALU.is_equal).then_inc(s_eq[h], 1)
                        for c in (2 * h, 2 * h + 1):
                            ins = dve.tensor_scalar(src_hot[c], iota[0:CE, 0:NSRC],
                                                    src_t[:, c, bass.ds(group, 1)], None, ALU.is_equal)
                        ins.then_inc(s_hot[h], 1)

            for w in range(NW):
                window_hots(w)
            dve.wait_ge(s_rw, 1)
            dve.tensor_tensor(rw_hl[:, :, 1, :], rw_sb[:, :, :], rw_hl[:, :, 0, :].bitcast(F32),
                              ALU.subtract).then_inc(s_rw, 1)
            for s in range(T + 2):
                t = s - 1
                if 0 <= t < T:
                    dve.wait_ge(s_yhi, t + 1)
                    for k in range(KF):
                        f, r = frows[k], rows[t]
                        ins = dve.tensor_tensor(yt_hl[1][0:f, k, 0:r], ps[2 + t % 2][0:f, 1, k * P:k * P + r],
                                                yt_hl[0][0:f, k, 0:r].bitcast(F32), ALU.subtract)
                    ins.then_inc(s_ylo, 1)
                if s < T:
                    r = rows[s]
                    dve.wait_ge(s_agg, s + 1)
                    if s >= 1:
                        dve.wait_ge(s_yt, s)
                    root_o, agg_o = agg_views(s)
                    for k in range(R):
                        v.mark(dve.tensor_scalar(cnt[0:r, k:k + 1], agg_o[k][-1][1][:, -1:], 1.0, None, ALU.max))
                    step(dve.tensor_tensor(z_sb[0:r, :], root_o, bias_row[0:r, :], ALU.add))
                    step(dve.reciprocal(inv[0:r, :], cnt[0:r, :]))
                    for k in range(R):
                        for at, o in agg_o[k]:
                            n = min(at + o.shape[1], F) - at
                            v.mark(dve.scalar_tensor_tensor(z_sb[0:r, at:at + n], o[:, 0:n], inv[0:r, k:k + 1],
                                                            z_sb[0:r, at:at + n], ALU.mult, ALU.add))
                        dve.wait_ge(s_v, v.n)
                    dve.tensor_scalar(m_sb[0:r, :], z_sb[0:r, :], 0.0, None, ALU.min).then_inc(s_m, 1)
                    step(dve.tensor_scalar(z_sb[0:r, :], z_sb[0:r, :], 0.0, None, ALU.max))
                    dve.wait_ge(s_e, s + 1)
                    dve.scalar_tensor_tensor(z_sb[0:r, :], e_sb[0:r, :], -1.0, z_sb[0:r, :],
                                             ALU.add, ALU.add).then_inc(s_y, 1)
                t = s - 1
                if 0 <= t < T:
                    r = rows[t]
                    dve.wait_ge(s_o, t + 1)
                    dve.wait_ge(s_xh, t + 1)
                    dve.tensor_tensor(y_acc[0:r, t, :], y_acc[0:r, t, :],
                                      ps[0][0:r, :, :].rearrange("p a n -> p (a n)"), ALU.add).then_inc(s_x2, 1)
                    stats(t, T + t, s_x2, t + 1)
                t = s - 2
                if 0 <= t < T:
                    split_rows_lo(t, T + t)

            def split_lo(pair, u):
                raw_v, hi_v, lo_v = unit_views(u)
                dve.wait_ge(s_hi, unit(pair, u) + 1)
                dve.tensor_tensor(lo_v, raw_v, hi_v.bitcast(F32), ALU.subtract).then_inc(s_lo, 1)

            def route():
                dve.wait_ge(s_g, 1)
                for n in range(2):
                    for t in range(T):
                        r, c = rows[t], (2 * t + n) * NE
                        other = rb_row[0:r, :] if n == 0 else gate[0:r, t, :]
                        v.mark(dve.tensor_tensor(gate[0:r, t, :], ps[3][0:r, 0, c:c + NE], other, ALU.add))
                    dve.wait_ge(s_v, v.n)
                for t in range(T):
                    v.mark(dve.max(top[:, t, :], gate[:, t, :]))
                dve.wait_ge(s_v, v.n)
                for t in range(T):
                    v.mark(dve.max_index(top_i[:, t, :], top[:, t, :], gate[:, t, :]))
                dve.wait_ge(s_v, v.n)
                step(dve.tensor_tensor(gd[:, :], top[:, :, 1], top[:, :, 0], ALU.subtract))
                dve.tensor_copy(top_f[:, :, :], top_i[:, :, 0:2]).then_inc(s_gd, 1)
                dve.wait_ge(s_ge, 1)
                step(dve.tensor_scalar(gs[:, :], ge[:, :], 1.0, None, ALU.add))
                step(dve.reciprocal(pr[:, 0, :], gs[:, :]))
                step(dve.tensor_tensor(pr[:, 1, :], pr[:, 0, :], ge[:, :], ALU.mult))

                ei = e_idx[:, :].rearrange("p (a e) -> p a e", a=1).to_broadcast([P, T, NE])
                for j in range(2):
                    tf = top_f[:, :, j:j + 1].to_broadcast([P, T, NE])
                    pj = pr[:, j, :].rearrange("p (t a) -> p t a", a=1).to_broadcast([P, T, NE])
                    step(dve.tensor_tensor(hot[:, j], tf, ei, ALU.is_equal))
                    step(dve.tensor_tensor(hot[:, j], hot[:, j], pj, ALU.mult))
                step(dve.memset(w_sb[:, :, NE:NX], 1.0 / NS))
                dve.tensor_tensor(w_sb[:, :, 0:NE], hot[:, 0], hot[:, 1], ALU.add).then_inc(s_w, 1)
                dve.wait_ge(s_w, 1)
                step(dve.tensor_copy(w_hl[:, 0], w_sb[:, :, :]))
                dve.tensor_tensor(w_hl[:, 1], w_sb[:, :, :], w_hl[:, 0].bitcast(F32), ALU.subtract).then_inc(s_wr, 1)

            def hidden_scale(pair, q, e):
                hq = 2 * KH * pair + q
                dve.wait_ge(f_g, hq + 1)
                if e is None:
                    dve.tensor_scalar(g_sb[q % 2], g_sb[q % 2], 1.0 / NS, None, ALU.mult).then_inc(f_m, 1)
                else:
                    row = wb[:, bass.ds(e + q // KH, 1), :].rearrange("p a n -> p (a n)") \
                        if not isinstance(e, int) else wb[:, e + q // KH, :]
                    dve.tensor_tensor(g_sb[q % 2], g_sb[q % 2], row, ALU.mult).then_inc(f_m, 1)

            def hidden_lo(pair, q):
                hq = 2 * KH * pair + q
                dve.wait_ge(f_hi, hq + 1)
                dve.tensor_tensor(ht_hl[1][:, q, :], g_sb[q % 2], ht_hl[0][:, q, :].bitcast(F32),
                                  ALU.subtract).then_inc(f_lo, 1)

            def add_block(pair, b):
                t, h = block_of(b)
                n = 2 * T * pair + b
                dve.wait_ge(f_y, n + 1)
                dve.wait_ge(f_acc, n - 2 * T + 1) if not isinstance(pair, int) or pair > 0 else None
                dve.tensor_tensor(y_acc[0:rows[t], t, h * DH:(h + 1) * DH], y_acc[0:rows[t], t, h * DH:(h + 1) * DH],
                                  ps[2 + b % 4 // 2][0:rows[t], b % 2, :], ALU.add).then_inc(f_acc, 1)

            def pair_dve(pair, e, last):
                split_lo(pair, 2)
                for q in range(2):
                    hidden_scale(pair, q, e)
                for q in range(2):
                    hidden_lo(pair, q)
                split_lo(pair, 3)
                if e is None:
                    route()
                for q in range(2, 4):
                    hidden_scale(pair, q, e)
                for q in range(2, 4):
                    hidden_lo(pair, q)
                if e is None:
                    dve.wait_ge(s_wt, 1)
                    dve.tensor_copy(w_t[:, 0:N], ps[0][0:NX, :, :].rearrange("p a n -> p (a n)")[:, 0:N]) \
                       .then_inc(s_wts, 1)
                for b in range(2 * T):
                    add_block(pair, b)
                    if not last and b in (1, 4):
                        split_lo(pair + 1, b // 3)

            step(dve.memset(wb[:, :, N + 1:NP], 0.0))
            split_lo(0, 0)
            split_lo(0, 1)
            pair_dve(0, None, False)
            dve.wait_ge(s_wbs, NE)
            with dve.Fori(0, NRP - 1) as i:
                pair_dve(i + 1, 2 * i, False)
            pair_dve(NRP, 2 * NRP - 2, True)

        @block.tensor
        def _(pe):
            def hilo(out_ap, parts, start=True, stop=True):
                n = 3 * len(parts)
                k = 0
                for (lh, ll), (rh, rl) in parts:
                    for a, b in ((lh, rh), (lh, rl), (ll, rh)):
                        ins = pe.matmul(out_ap, a, b, start=start and k == 0, stop=stop and k == n - 1)
                        k += 1
                return ins

            for used in (*s_used, *s_eq):
                pe.sem_inc(used, 1)
            pe.wait_ge(s_const, N_CONST)
            pe.wait_ge(s_kf, 1)
            for n, v in enumerate((key_f, src_f)):
                for j in range(CG):
                    c = (CG * n + j) * G
                    pe.transpose(ps[2][0:CE, 0, c:c + G], v[:, j * CE:(j + 1) * CE], ident[0:G, 0:G])
            for n in range(2):
                ins = pe.matmul(ps[3][0:NW, 0, n * G:(n + 1) * G], kmm_b[:, n, :], ident[0:G, 0:G],
                                start=True, stop=True)
            ins.then_inc(s_kt, 1)
            pe.wait_ge(s_b1, 32)
            pe.transpose(ps[2][:, 1, 0:NX * KH], b1_rows[:, :], ident[0:NX * KH, 0:NX * KH]).then_inc(s_bt, 1)

            def rows_t(source, ready, t, n):
                pe.wait_ge(ready, t + 1)
                if n >= 2:
                    pe.wait_ge(s_xlo, n - 1 if n < T else n)
                for k in range(KD):
                    ins = pe.transpose(ps_rows(n)[:, k, 0:rows[t]], source[t % 2][0:rows[t], k * P:(k + 1) * P],
                                       ident[0:rows[t], 0:rows[t]])
                ins.then_inc(s_xr, 1)

            for t in range(2):
                rows_t(xn, s_n, t, t)
            pe.wait_ge(s_rng, 1)
            pe.matmul(ps[3][0:1, 1, 0:NW], rng[:, 2:3], ident[0:NW, 0:NW], start=True, stop=True)
            pe.matmul(ps[3][0:1, 1, NW:2 * NW], rng[:, 3:4], ident[0:NW, 0:NW], start=True, stop=True)
            pe.matmul(ps[3][0:1, 1, 2 * NW:3 * NW], rng[:, 3:4], tri[:, :], start=True, stop=True).then_inc(s_rt, 1)
            def project(t, r):
                cols = slice(t * P, t * P + rows[t])
                return hilo(ps[h_bank(t)][0:rows[t], r, 0:F],
                            [((xt[:, 0, k, cols], xt[:, 1, k, cols]), (rel_hl[0][:, r, k], rel_hl[1][:, r, k]))
                             for k in range(KD)])

            for t in range(2, T):
                rows_t(xn, s_n, t, t)
                if t < 4:
                    pe.wait_ge(s_xlo, t - 1)
                    if t == 2:
                        pe.wait_ge(s_win, 1)
                        pe.wait_ge(s_lo, R)
                    else:
                        pe.wait_ge(s_b1t, 1)
                    for r in range(R):
                        ins = project(t - 2, r)
                    ins.then_inc(s_h, 1)
            pe.wait_ge(s_xlo, T)

            def window_counts(w):
                first, number, before = window_regs(pe, win, NW, w, G)
                u = w % 2
                if w >= 2:
                    pe.wait_ge(s_at, w - 1)
                full, last = ps[u][:, 0, 0:(T - 1) * WK], ps[u][:, 1, 0:WK]
                for o in (full, last):
                    pe.matmul(o, zeros[:, 0:P], zeros[:, 0:o.shape[1]], start=True, stop=False)
                with pe.Fori(0, number) as j:
                    for h in range(2):
                        pe.wait_ge(s_hot[h], before + j + 1)
                        for c in (2 * h, 2 * h + 1):
                            for s in range(T):
                                o = full[:, s * WK:(s + 1) * WK] if s < T - 1 else last
                                ins = pe.matmul(o, src_hot[c][:, s * P:(s + 1) * P], key_hot[:, c, :],
                                                start=False, stop=False)
                        ins.then_inc(s_used[h], 1)
                for o in (full, last):
                    ins = pe.matmul(o, zeros[:, 0:P], zeros[:, 0:o.shape[1]], start=False, stop=True)
                ins.then_inc(s_c, 1)

            for w in range(NW):
                window_counts(w)
                t, r = projected(w)
                if t is not None:
                    if t >= 2:
                        pe.wait_ge(s_hs, t - 1)
                    ins = project(t, r)
                    if r == R - 1:
                        ins.then_inc(s_h, 1)

            def root(t):
                if t >= 2:
                    pe.wait_ge(s_ylo, t - 1)
                cols = slice(t * P, t * P + rows[t])
                hilo(agg_views(t)[0], [((xt[:, 0, k, cols], xt[:, 1, k, cols]), (root_hl[0][:, k], root_hl[1][:, k]))
                                       for k in range(KD)])

            def aggregate(t, r):
                cols = slice(t * P, t * P + rows[t])
                for at, o in agg_views(t)[1][r]:
                    for s in range(T):
                        ins = pe.matmul(o, a_t[0:rows[s], s, r, cols], h_rel[s][0:rows[s], r, at:at + o.shape[1]],
                                        start=(s == 0), stop=(s == T - 1))
                return ins

            def elu_t(t):
                pe.wait_ge(s_y, t + 1)
                for k in range(KF):
                    ins = pe.transpose(ps[2 + t % 2][0:frows[k], 1, k * P:k * P + rows[t]],
                                       z_sb[0:rows[t], k * FK:k * FK + frows[k]], ident[0:rows[t], 0:rows[t]])
                ins.then_inc(s_yt, 1)

            def output(t):
                pe.wait_ge(s_ylo, t + 1)
                if t >= 1:
                    pe.wait_ge(s_x2, t)
                for h in range(2):
                    ins = hilo(ps[0][0:rows[t], h, :],
                               [((yt_hl[0][0:frows[k], k, 0:rows[t]], yt_hl[1][0:frows[k], k, 0:rows[t]]),
                                 (wo_hl[0][0:frows[k], k, h * DH:(h + 1) * DH],
                                  wo_hl[1][0:frows[k], k, h * DH:(h + 1) * DH])) for k in range(KF)])
                ins.then_inc(s_o, 1)

            def gates(t):
                pe.wait_ge(s_xlo, T + t + 1)
                for k in range(KD):
                    for n in range(2):
                        ins = pe.matmul(ps[3][0:rows[t], 0, 2 * t * NE:2 * (t + 1) * NE],
                                        xt[:, n, k, t * P:t * P + rows[t]],
                                        rw_hl[:, k, :, :].rearrange("p a e -> p (a e)"),
                                        start=(k == 0 and n == 0), stop=(k == KD - 1 and n == 1))
                return ins

            pe.wait_ge(s_lo, NG)
            pe.wait_ge(s_at, NW)
            pe.wait_ge(s_hs, T)
            pe.wait_ge(s_ones, T)
            for s in range(T + 1):
                if s < T:
                    root(s)
                    aggregate(s, 0)
                if s >= 1:
                    elu_t(s - 1)
                if s < T:
                    aggregate(s, 1).then_inc(s_agg, 1)
                if s == T:
                    rows_t(x3, s_x3, T - 2, 2 * T - 2)
                if s >= 1:
                    output(s - 1)
                if 2 <= s < T:
                    rows_t(x3, s_x3, s - 2, T + s - 2)
            pe.wait_ge(s_rw, 2)
            for t in range(T - 1):
                gates(t)
            rows_t(x3, s_x3, T - 1, 2 * T - 1)
            gates(T - 1).then_inc(s_g, 1)

            def up_expert(pair, e):
                pe.wait_ge(s_lo, unit(pair, e) + 1)
                for m in range(KH):
                    q = KH * e + m
                    hq = 2 * KH * pair + q
                    if not isinstance(pair, int) or hq >= 2:
                        pe.wait_ge(f_g, hq - 1)
                    for a in range(2):
                        ins = hilo(ps[q % 2][:, a, 0:NL],
                                   [((w1_hl[0][:, e, k, m * P:(m + 1) * P], w1_hl[1][:, e, k, m * P:(m + 1) * P]),
                                     (xt[:, 0, k, a * NL:(a + 1) * NL], xt[:, 1, k, a * NL:(a + 1) * NL]))
                                    for k in range(KD)])
                    ins.then_inc(f_h, 1)

            def down_pair(pair, bias):
                def part(b, experts, start, stop):
                    t, h = block_of(b)
                    cols = slice(t * P, t * P + rows[t])
                    return hilo(ps[2 + b % 4 // 2][0:rows[t], b % 2, :],
                                [((ht_hl[0][:, KH * e + m, cols], ht_hl[1][:, KH * e + m, cols]),
                                  (w2_hl[0][:, e, m, h * DH:(h + 1) * DH], w2_hl[1][:, e, m, h * DH:(h + 1) * DH]))
                                 for e in experts for m in range(KH)], start=start, stop=stop)

                def opened(b):
                    n = 2 * T * pair + b
                    if not isinstance(n, int) or n >= 4:
                        pe.wait_ge(f_acc, n - 1 if b < 2 else n - 3)
                    return True

                pe.wait_ge(s_lo, unit(pair, 2) + 1)
                pe.wait_ge(f_lo, 2 * KH * pair + KH)
                if bias:
                    pe.wait_ge(s_gd, 1)
                for b in range(4):
                    part(b, (0,), opened(b), False)
                if bias:
                    pe.wait_ge(s_w, 1)
                    pe.wait_ge(f_g, 2 * KH)
                    for t in range(T):
                        ins = pe.transpose(ps[0][:, :, :].rearrange("p a n -> p (a n)")
                                           [0:NX, t * P:t * P + rows[t]],
                                           w_sb[0:rows[t], t, :], ident[0:rows[t], 0:rows[t]])
                    ins.then_inc(s_wt, 1)
                pe.wait_ge(s_lo, unit(pair, 3) + 1)
                pe.wait_ge(f_lo, 2 * KH * pair + 2 * KH)
                for b in range(2 * T):
                    ins = part(b, (1,) if b < 4 else (0, 1), b >= 4 and opened(b), not bias)
                    if bias:
                        t, h = block_of(b)
                        if b == 0:
                            pe.wait_ge(s_wts, 1)
                            pe.wait_ge(s_b2, 32)
                        ins = pe.matmul(ps[2 + b % 4 // 2][0:rows[t], b % 2, :], w_t[:, t * P:t * P + rows[t]],
                                        b2_sb[:, h * DH:(h + 1) * DH], start=False, stop=True)
                    ins.then_inc(f_y, 1)
                    if bias and 1 <= b <= NE:
                        spread(b - 1)

            def spread(e):
                if e == 0:
                    pe.wait_ge(s_wr, 1)
                    pe.wait_ge(s_b1t, 2)
                if e >= 2:
                    pe.wait_ge(s_wbs, e - 1)
                for t in range(T):
                    n = rows[t] + rows[t] % 2
                    for h in range(2):
                        ins = pe.matmul(wb_bank(e)[:, t * P:t * P + n],
                                        w_hl[0:rows[t], h, t, e:e + 1].to_broadcast([rows[t], P]),
                                        ident_r[0:rows[t], 0:n], start=(h == 0), stop=(h == 1))
                ins.then_inc(s_wb, 1)

            def pair_pe(pair):
                up_expert(pair, 0)
                up_expert(pair, 1)
                down_pair(pair, False)

            up_expert(0, 0)
            up_expert(0, 1)
            down_pair(0, True)
            pe.wait_ge(s_wbs, NE)
            with pe.Fori(0, NRP) as i:
                pair_pe(i + 1)
    return nc


INS = ["x", "src", "dst", "edge_type_2", "L0_gnn_ln_weight", "L0_gnn_W_rel", "L0_gnn_W_root", "L0_gnn_conv_bias",
       "L0_gnn_wo_weight", "L0_ffn_rW", "L0_ffn_rb", "L0_ffn_W1", "L0_ffn_b1", "L0_ffn_W2", "L0_ffn_b2",
       "L0_ffn_sW1", "L0_ffn_sb1", "L0_ffn_sW2", "L0_ffn_sb2"]


def kernel(**inputs):
    import numpy as np
    import concourse.bacc as bacc
    from concourse.bass_utils import run_bass_kernel_spmd

    nc = bacc.Bacc("TRN2", target_bir_lowering=False, num_devices=1)
    arrays, args = {}, []
    for name in INS:
        a = np.ascontiguousarray(inputs[name])
        arrays[f"in_{name}"] = a
        args.append(nc.dram_tensor(f"in_{name}", a.shape, mybir.dt.from_np(a.dtype), kind="ExternalInput").ap())
    out = nc.dram_tensor("out", inputs["x"].shape, F32, kind="ExternalOutput").ap()
    program(nc, *args, out)
    return run_bass_kernel_spmd(nc, [arrays], core_ids=[0]).results[0]["out"]
```

```python
import concourse.bass as bass
from concourse import mybir
from contextlib import ExitStack

F32 = mybir.dt.float32
F32R = mybir.dt.float32r
F16 = mybir.dt.float16
I32 = mybir.dt.int32
U32 = mybir.dt.uint32
ALU = mybir.AluOpType
ACT = mybir.ActivationFunctionType
AX = mybir.AxisListType


class Tally:

    def __init__(self, sem):
        self.sem, self.n, self.off = sem, 0, 0

    def mark(self, ins):
        ins.then_inc(self.sem, 1)
        self.n += 1
        return self.n + self.off

    def now(self):
        return self.n + self.off


def program(nc, x, src, dst, rel, ln_w, w_rel, w_root, conv_b, wo, rw, rb, w1, b1, w2, b2, sw1, sb1, sw2, sb2, out):
    N, D = x.shape
    E = src.shape[0]
    R, _, F = w_rel.shape
    NE, _, HID = w1.shape
    NS = sw1.shape[0]
    NX = NE + NS
    P = 128
    T = -(-N // P)
    rows = [min(P, N - t * P) for t in range(T)]
    KD = D // P
    KH = HID // P
    NP = 628
    NL = NP // 2
    CE = 125
    CG = 4
    EG = CG * CE
    G = E // EG
    assert G * EG == E
    H_PARTS = 4
    assert H_PARTS <= G
    KEYS = R * N
    WK = 126
    WD = WK // R
    NW = -(-KEYS // WK)
    ND = NW * WD
    assert NW * WK <= 2048
    NSRC = T * P
    FK = 96
    KF = -(-F // FK)
    frows = [min(FK, F - k * FK) for k in range(KF)]
    DH = D // 2

    ctx = ExitStack()
    with ctx:
        def sb(name, shape, dt=F32):
            return ctx.enter_context(nc.sbuf_tensor(name, shape, dt))

        def sem(name):
            return ctx.enter_context(nc.semaphore(name))

        xt = sb("xt", [P, 2, KD, NP], F32R)
        y_acc = sb("y_acc", [P, T, D])
        ident = sb("ident", [P, P])
        W_REL, W_ROOT, W_O = R * KD * F, KD * F, KF * D
        UNIT = KD * HID
        assert UNIT == KH * D
        arena_r = sb("arena_r", [P, 8 * UNIT + 4 * KH * NP], F32R)
        at = 0

        def cut(n):
            nonlocal at
            at += n
            return arena_r[:, at - n:at]
        rel_hl = [cut(W_REL).rearrange("p (r k f) -> p r k f", r=R, k=KD) for _ in range(2)]
        root_hl = [cut(W_ROOT).rearrange("p (k f) -> p k f", k=KD) for _ in range(2)]
        wo_hl = [cut(W_O).rearrange("p (k n) -> p k n", k=KF) for _ in range(2)]
        yt_hl = [cut(KF * P).rearrange("p (k n) -> p k n", k=KF) for _ in range(2)]
        assert at <= arena_r.shape[1]
        at = 0
        w1_hl = [cut(2 * UNIT).rearrange("p (e k n) -> p e k n", e=2, k=KD) for _ in range(2)]
        w2_hl = [cut(2 * UNIT).rearrange("p (e k n) -> p e k n", e=2, k=KH) for _ in range(2)]
        ht_hl = [cut(2 * KH * NP).rearrange("p (q n) -> p q n", q=2 * KH) for _ in range(2)]
        big = sb("big", [P, max(T * R * ND, NX * NP)])
        h0 = [big[:, i * D:(i + 1) * D] for i in range(2)]
        xn = [big[:, (2 + i) * D:(3 + i) * D] for i in range(2)]
        dst_i, rel_i = (big[0:G, 5 * D + i * EG:5 * D + (i + 1) * EG].bitcast(I32) for i in range(2))
        assert 5 * D + 2 * EG <= big.shape[1]
        lnw_row = big[:, 4 * D:5 * D]
        a_t = big[:, 0:T * R * ND].rearrange("p (s r d) -> p s r d", s=T, r=R)
        wb = big[:, 0:NX * NP].rearrange("p (e n) -> p e n", e=NX)
        SLOT = KD * F
        raw = sb("raw", [P, 2 * SLOT])
        slot = [raw[:, i * SLOT:(i + 1) * SLOT] for i in range(2)]
        HF = F + 2
        h_at = {0: SLOT - 2 * R * HF, 1: SLOT - R * HF, 2: 0, 3: SLOT, 4: SLOT + R * HF}
        assert T == len(h_at) and 3 * R * HF <= SLOT and SLOT - 2 * R * HF >= D
        h_rel = [raw[:, h_at[t]:h_at[t] + R * HF].rearrange("p (r f) -> p r f", r=R) for t in range(T)]
        work = sb("work", [P, 2 * D])
        src_i = work[0:G, 0:EG].bitcast(I32)
        key_f = work[0:G, EG:2 * EG]
        src_f = work[0:G, 2 * EG:3 * EG]
        hot_at = CG * WK // 2
        key_hot = work[0:CE, 0:hot_at].bitcast(F16).rearrange("p (c k) -> p c k", c=CG)
        src_hot = [work[0:CE, hot_at + c * NSRC // 2:hot_at + (c + 1) * NSRC // 2].bitcast(F16) for c in range(CG)]
        dif_at = hot_at + CG * NSRC // 2
        key_dif = work[0:CE, dif_at:dif_at + CG * WK // 2].bitcast(F16).rearrange("p (c k) -> p c k", c=CG)
        assert dif_at + CG * WK // 2 <= 2 * D
        x3 = [work[:, i * D:(i + 1) * D] for i in range(2)]
        g_sb = [work[:, i * NP:(i + 1) * NP] for i in range(2)]
        late = sb("late", [P, D])
        iota = late[:, 0:NW * WK // 2].bitcast(F16)
        b2_sb = late[0:NX, :]
        mid = sb("mid", [P, 3 * F])
        z_sb, m_sb, e_sb = (mid[:, i * F:(i + 1) * F] for i in range(3))
        w_t = mid[0:NX, 0:NP]
        g_t = mid[0:2 * NE, 0:NP]
        key_t = mid[0:CE, 0:CG * G].rearrange("p (j g) -> p j g", j=CG)
        src_t = mid[0:CE, CG * G:2 * CG * G].rearrange("p (j g) -> p j g", j=CG)
        bias_row = sb("bias_row", [P, F])
        rw_sb = sb("rw_sb", [P, KD, NE])
        rw_hl = sb("rw_hl", [P, KD, 2, NE], F32R)
        ident_r = sb("ident_r", [P, P], F32R)
        w_hl = sb("w_hl", [P, 2, T, NX], F32R)
        rb_row = sb("rb_row", [P, NE])
        b1_rows = sb("b1_rows", [NX * KH, P])
        b1_t = sb("b1_t", [P, NX * KH])
        zeros = sb("zeros", [1, 512], F16)
        st = sb("st", [P, 2, 6])
        mv = sb("mv", [P, T, 2])
        rstd = sb("rstd", [P, T])
        minus_half = sb("minus_half", [P, 1])
        rstd_1 = sb("rstd_1", [P, T])
        nmr = sb("nmr", [P, T])
        sumsq = sb("sumsq", [P, T])
        rms = sb("rms", [P, T])
        kmm = sb("kmm", [G, 2])
        kmm_b = sb("kmm_b", [G, 2, NW])
        first_key = sb("first_key", [NW, 1])
        last_key = sb("last_key", [NW, 1])
        down, up, act_a, act_b = (late[0:NW, D - (i + 1) * G:D - i * G] for i in range(4))
        rng = sb("rng", [NW, 4])
        win = sb("win", [1, 2 * NW], I32)
        cnt = sb("cnt", [P, R])
        inv = sb("inv", [P, R])
        gate = sb("gate", [P, T, NE])
        top = sb("top", [P, T, 8])
        top_i = sb("top_i", [P, T, 8], U32)
        top_f = sb("top_f", [P, T, 2])
        gd = sb("gd", [P, T])
        ge = sb("ge", [P, T])
        gs = sb("gs", [P, T])
        pr = sb("pr", [P, 2, T])
        hot = sb("hot", [P, 2, T, NE])
        e_idx = sb("e_idx", [P, NE])
        w_sb = sb("w_sb", [P, T, NX])

        ps = [ctx.enter_context(nc.psum_tensor(f"ps{i}", [P, 2, 512], F32)) for i in range(4)]

        def ps_rows(n):
            return ps[n % 2 if n < T else 1][:, :, :].rearrange("p a (b c) -> p (a b) c", c=P)

        s_x = [sem(f"s_xin{t}") for t in range(T)]
        s_edge = sem("s_edge")
        s_lnw = sem("s_lnw")
        s_convb = sem("s_convb")
        s_small = sem("s_small")
        s_b1 = sem("s_b1")
        s_b2 = sem("s_b2")
        s_raw = [sem(f"s_raw{i}") for i in range(2)]
        s_const = sem("s_const")
        s_hi = sem("s_hi")
        s_lo = sem("s_lo")
        s_v = sem("s_v")
        s_a = sem("s_a")
        s_kf = sem("s_kf")
        s_kt = sem("s_kt")
        s_rng = sem("s_rng")
        s_rt = sem("s_rt")
        s_win = sem("s_win")
        s_ln = sem("s_ln")
        s_p = sem("s_p")
        s_mv = sem("s_mv")
        s_rms = sem("s_rms")
        s_h0 = sem("s_h0")
        s_xh = sem("s_xh")
        s_n = sem("s_n")
        s_xr = sem("s_xr")
        s_xhi = sem("s_xhi")
        s_xlo = sem("s_xlo")
        s_hot = [sem(f"s_hot{u}") for u in range(2)]
        s_used = [sem(f"s_used{u}") for u in range(2)]
        s_dif = [sem(f"s_dif{u}") for u in range(2)]
        s_eq = [sem(f"s_eq{u}") for u in range(2)]
        s_c = sem("s_c")
        s_ones = sem("s_ones")
        s_at = sem("s_at")
        s_h = sem("s_h")
        s_hs = sem("s_hs")
        s_agg = sem("s_agg")
        s_m = sem("s_m")
        s_e = sem("s_e")
        s_y = sem("s_y")
        s_yt = sem("s_yt")
        s_yhi = sem("s_yhi")
        s_ylo = sem("s_ylo")
        s_o = sem("s_o")
        s_x2 = sem("s_xtwo")
        s_x3 = sem("s_xthree")
        s_rw = sem("s_rw")
        s_b1t = sem("s_b1t")
        s_bt = sem("s_bt")
        s_gt = sem("s_gt")
        s_gts = sem("s_gts")
        s_slot1 = sem("s_slot1")
        s_g = sem("s_g")
        s_wr = sem("s_wr")
        s_gd = sem("s_gd")
        s_ge = sem("s_ge")
        s_w = sem("s_w")
        s_wt = sem("s_wt")
        s_wts = sem("s_wts")
        s_wb = sem("s_wb")
        s_wbs = sem("s_wbs")
        f_h = sem("f_h")
        f_g = sem("f_g")
        f_m = sem("f_m")
        f_hi = sem("f_hi")
        f_lo = sem("f_lo")
        f_y = sem("f_y")
        f_acc = sem("f_acc")
        s_out = sem("s_out")

        NG = 5
        NPAIR = NX // 2
        NRP = NE // 2

        def unit(pair, u):
            return NG + 4 * pair + u

        def w_slot(u):
            return (NG + u) % 2

        block = ctx.enter_context(nc.Block())

        @block.sync
        def _(sp):
            def load_x(t):
                sp.dma_start(y_acc[0:rows[t], t, :], x[t * P:t * P + rows[t], :]).then_inc(s_x[t], 16)

            def raw_free(n):
                if not isinstance(n, int) or n >= 2:
                    sp.wait_ge(s_lo, n - 1)

            load_x(0)
            load_x(1)
            sp.dma_start(lnw_row, ln_w.rearrange("(a n) -> a n", a=1).to_broadcast([P, D])).then_inc(s_lnw, 16)
            for t in range(2, T):
                load_x(t)
            for n in range(R):
                sp.dma_start(slot[n].rearrange("p (k f) -> p k f", k=KD),
                             w_rel[n].rearrange("(k p) f -> p k f", p=P)).then_inc(s_raw[n], 16)
            sp.dma_start(bias_row[:, :], conv_b.rearrange("(a n) -> a n", a=1).to_broadcast([P, F])).then_inc(s_convb, 16)
            raw_free(2)
            sp.dma_start(slot[0].rearrange("p (k f) -> p k f", k=KD),
                         w_root.rearrange("(k p) f -> p k f", p=P)).then_inc(s_raw[0], 16)
            raw_free(3)
            sp.dma_start(slot[1][0:FK, 0:2 * D].rearrange("p (k n) -> p k n", k=2),
                         wo[0:2 * FK, :].rearrange("(k p) n -> p k n", p=FK)).then_inc(s_raw[1], 16)
            raw_free(4)
            sp.dma_start(slot[0][0:frows[2], 0:D], wo[2 * FK:F, :]).then_inc(s_raw[0], 16)
            sp.dma_start(rw_sb[:, :, :], rw.rearrange("(k p) e -> p k e", p=P)).then_inc(s_small, 16)
            sp.dma_start(rb_row[:, :], rb.rearrange("(a n) -> a n", a=1).to_broadcast([P, NE])).then_inc(s_small, 16)
            sp.wait_ge(s_c, NW)
            sp.dma_start(b2_sb[0:NE, :], b2).then_inc(s_b2, 16)
            sp.dma_start(b2_sb[NE:NX, :], sb2).then_inc(s_b2, 16)
            def load_pair(w1s, w2s, pair):
                for u in range(4):
                    if isinstance(pair, int) and u < 2:
                        sp.wait_ge(*((s_slot1, 1) if w_slot(u) == 1 else (s_agg, T)))
                    raw_free(unit(pair, u))
                    s = w_slot(u)
                    if u < 2:
                        sp.dma_start(slot[s][:, 0:UNIT].rearrange("p (k n) -> p k n", k=KD),
                                     w1s(u)).then_inc(s_raw[s], 16)
                    else:
                        sp.dma_start(slot[s][:, 0:UNIT].rearrange("p (k n) -> p k n", k=KH),
                                     w2s(u - 2)).then_inc(s_raw[s], 16)

            load_pair(lambda e: sw1[e].rearrange("(k p) n -> p k n", p=P),
                      lambda e: sw2[e].rearrange("(k p) n -> p k n", p=P), 0)
            w1v = w1.rearrange("e (k p) n -> e p k n", p=P)
            w2v = w2.rearrange("e (k p) n -> e p k n", p=P)
            with sp.Fori(0, NRP) as i:
                load_pair(lambda e: w1v[bass.ds(2 * i + e, 1)].rearrange("e p k n -> (e p) k n"),
                          lambda e: w2v[bass.ds(2 * i + e, 1)].rearrange("e p k n -> (e p) k n"), i + 1)
            for t in range(T):
                sp.wait_ge(f_acc, 2 * T * (NPAIR - 1) + 2 * t + 2)
                sp.dma_start(out[t * P:t * P + rows[t], :], y_acc[0:rows[t], t, :]).then_inc(s_out, 16)
            sp.wait_ge(s_out, 16 * T)

        N_CONST = 12

        def kf2(v, n):
            return v.rearrange("p (k n) -> p k n", k=n)
        gnn_units = [(kf2(slot[0], KD), rel_hl[0][:, 0], rel_hl[1][:, 0]),
                     (kf2(slot[1], KD), rel_hl[0][:, 1], rel_hl[1][:, 1]),
                     (kf2(slot[0], KD), root_hl[0], root_hl[1]),
                     (kf2(slot[1][0:FK, 0:2 * D], 2), wo_hl[0][0:FK, 0:2], wo_hl[1][0:FK, 0:2]),
                     (slot[0][0:frows[2], 0:D], wo_hl[0][0:frows[2], 2], wo_hl[1][0:frows[2], 2])]

        def unit_lo(eng, n):
            raw_v, hi_v, lo_v = gnn_units[n]
            eng.wait_ge(s_hi, n + 1)
            eng.tensor_tensor(lo_v, raw_v, hi_v.bitcast(F32), ALU.subtract).then_inc(s_lo, 1)

        def next_regs(eng, w, window=None, needs_first=True):
            if w + 1 == NW:
                return None
            first = eng.value_load(win[0:1, w + 1:w + 2], min_val=0, max_val=G - H_PARTS) if needs_first else None
            number = eng.value_load(win[0:1, NW + w + 1:NW + w + 2], min_val=H_PARTS, max_val=G)
            return first, number, 0 if window is None else window[2] + window[1]

        def group_of(first, j):
            return nc.s_assert_within(
                first + j, 0, G - 1, skip_runtime_bounds_check_because=
                "first + number is the end of the window's range, at most G whatever the keys are")

        @block.gpsimd
        def _(pool):
            k = Tally(s_const)
            k.mark(pool.memset(ident[:, :], 0.0))
            k.mark(pool.iota(iota, [[1, NW * WK]], base=0, channel_multiplier=0,
                             allow_small_or_imprecise_dtypes=True))
            k.mark(pool.iota(first_key[:, :], [[0, 1]], base=0, channel_multiplier=WK,
                             allow_small_or_imprecise_dtypes=True))
            k.mark(pool.iota(last_key[:, :], [[0, 1]], base=WK - 1, channel_multiplier=WK,
                             allow_small_or_imprecise_dtypes=True))
            k.mark(pool.iota(down, [[-1, G]], base=G, channel_multiplier=0,
                             allow_small_or_imprecise_dtypes=True))
            k.mark(pool.iota(up, [[1, G]], base=1, channel_multiplier=0,
                             allow_small_or_imprecise_dtypes=True))
            k.mark(pool.iota(e_idx[:, :], [[1, NE]], base=0, channel_multiplier=0,
                             allow_small_or_imprecise_dtypes=True))
            k.mark(pool.memset(zeros[:, :], 0.0))
            k.mark(pool.memset(xt[:, :, :, N:NP].bitcast(F32), 0.0))
            k.mark(pool.memset(gate[:, :, :], 0.0))
            k.mark(pool.memset(minus_half[:, :], -0.5))
            pool.wait_ge(s_const, 1)
            k.mark(pool.affine_select(out=ident[:, :], in_=ident[:, :], compare_op=ALU.not_equal, fill=1.0,
                                      base=0, pattern=[[-1, P]], channel_multiplier=1))
            assert k.n == N_CONST
            own = Tally(s_p)
            pool.wait_ge(s_const, N_CONST)

            def row_scale(t, n):
                r = rows[t]
                pool.wait_ge(s_mv, n + 1)
                own.mark(pool.tensor_scalar(rstd[0:r, t:t + 1], mv[0:r, t, 1:2], 1.0, 1e-5, ALU.mult, ALU.add))
                pool.wait_ge(s_p, own.n)
                own.mark(pool.tensor_tensor(rstd[0:r, t:t + 1], rstd[0:r, t:t + 1], minus_half[0:r, :], ALU.pow))
                pool.wait_ge(s_p, own.n)
                if n < T:
                    own.mark(pool.tensor_scalar(rstd_1[0:r, t:t + 1], rstd[0:r, t:t + 1], 1.0, 1.0,
                                                ALU.mult, ALU.add))
                pool.tensor_scalar(nmr[0:r, t:t + 1], mv[0:r, t, 0:1], rstd[0:r, t:t + 1], -1.0,
                                   ALU.mult, ALU.mult).then_inc(s_ln, 1)

            row_scale(0, 0)
            for t in range(T):
                r = rows[t]
                if t + 1 < T:
                    row_scale(t + 1, t + 1)
                pool.wait_ge(s_h0, t + 1)
                own.mark(pool.tensor_scalar(rms[0:r, t:t + 1], sumsq[0:r, t:t + 1], 1.0 / D, 1e-6,
                                            ALU.mult, ALU.add))
                pool.wait_ge(s_p, own.n)
                pool.tensor_tensor(rms[0:r, t:t + 1], rms[0:r, t:t + 1], minus_half[0:r, :],
                                   ALU.pow).then_inc(s_rms, 1)
            pool.wait_ge(s_lo, 2)
            for n in range(2, NG):
                unit_lo(pool, n)
            pool.wait_ge(s_lo, NG)
            for t in range(T):
                pool.memset(h_rel[t][:, :, F:HF], 1.0).then_inc(s_ones, 1)
            for t in range(T):
                r = rows[t]
                pool.tensor_scalar(y_acc[0:r, t, :], y_acc[0:r, t, :], rstd_1[0:r, t:t + 1], nmr[0:r, t:t + 1],
                                   ALU.mult, ALU.add).then_inc(s_xh, 1)
            for t in range(T):
                row_scale(t, T + t)

        def unit_views(u):
            raw_v = slot[w_slot(u)][:, 0:UNIT]
            if u < 2:
                return [kf2(raw_v, KD)] + [w[:, u] for w in w1_hl]
            return [kf2(raw_v, KH)] + [w[:, u - 2] for w in w2_hl]

        def h_bank(t):
            return 3 - t % 2

        h_steps = [(t, r, k) for t in range(2, T) for r in range(R) for k in range(KD)]
        h_slots = H_PARTS * (NW - 2)

        def steps_of(slot):
            return h_steps[len(h_steps) * slot // h_slots:len(h_steps) * (slot + 1) // h_slots]

        def tiles_done(w):
            return [t for part in range(H_PARTS) for t, r, k in steps_of(H_PARTS * (w - 1) + part)
                    if (r, k) == (R - 1, KD - 1)] if 1 <= w <= NW - 2 else []

        def agg_views(t):
            bank = ps[2 + t % 2][0:rows[t]]
            cut = 512 - (F + 1)
            return bank[:, 0, 0:F], [[(0, bank[:, 1, 0:F + 1])],
                                     [(0, bank[:, 1, F + 1:512]), (cut, bank[:, 0, F:2 * F + 1 - cut])]]

        def hidden_bank(pair, q):
            return ps[3 - q] if isinstance(pair, int) and pair == 0 and q < 2 else ps[q % 2]

        def wb_bank(e):
            return ps[(e + 1) % 2][:, :, :].rearrange("p a n -> p (a n)")

        def block_of(b):
            return b // 2, b % 2

        @block.scalar
        def _(act):
            v = Tally(s_a)
            for to, frm in ((dst_i, dst), (rel_i, rel), (src_i, src)):
                act.dma_start(to, frm.rearrange("(p e) -> p e", e=EG)).then_inc(s_edge, 16)
            act.dma_start(b1_rows[0:NE * KH, :], b1.rearrange("e (m p) -> (e m) p", p=P)).then_inc(s_b1, 16)
            act.dma_start(b1_rows[NE * KH:NX * KH, :], sb1.rearrange("e (m p) -> (e m) p", p=P)).then_inc(s_b1, 16)

            def split_rows(t, n):
                act.wait_ge(s_xr, n + 1)
                act.activation(xt[:, 0, :, t * P:t * P + rows[t]],
                               ps_rows(n)[:, :, 0:rows[t]], ACT.Copy).then_inc(s_xhi, 1)

            def unit_hi(n):
                raw_v, hi_v, _ = gnn_units[n]
                act.wait_ge(s_raw[n % 2], 16 * (n // 2 + 1))
                act.activation(hi_v, raw_v, ACT.Copy).then_inc(s_hi, 1)

            def h_out(t):
                act.wait_ge(s_h, t + 1)
                act.wait_ge(s_lo, 3 if t < 2 else NG)
                act.activation(h_rel[t][0:rows[t], :, 0:F], ps[h_bank(t)][0:rows[t], :, 0:F], ACT.Copy).then_inc(s_hs, 1)

            for s in range(T + 1):
                if s < T:
                    t, r = s, rows[s]
                    act.wait_ge(s_ln, t + 1)
                    if t >= 2:
                        act.wait_ge(s_xr, t - 1)
                        act.wait_ge(s_n, t - 1)
                    v.mark(act.activation(h0[t % 2][0:r, :], y_acc[0:r, t, :], ACT.Identity,
                                          bias=nmr[0:r, t:t + 1], scale=rstd[0:r, t:t + 1]))
                    act.wait_ge(s_a, v.n)
                    act.activation(xn[t % 2][0:r, :], h0[t % 2][0:r, :], ACT.Square,
                                   accum_out=sumsq[0:r, t:t + 1]).then_inc(s_h0, 1)
                if s == 1:
                    unit_hi(0)
                if s >= 1:
                    split_rows(s - 1, s - 1)
                if s in (1, 4):
                    unit_hi(1 + s // 4)
                if s == T - 1:
                    act.wait_ge(s_win, 1)
                    window_next = next_regs(act, -1)
                if s == 2:
                    act.wait_ge(s_bt, 1)
                    act.activation(b1_t[:, :], ps[2][:, 1, 0:NX * KH], ACT.Copy).then_inc(s_b1t, 1)
            act.wait_ge(s_n, T)

            def window_difs(w, window):
                first, number, before = window
                with act.Fori(0, number) as j:
                    group = group_of(first, j)
                    for h in range(2):
                        act.wait_ge(s_eq[h], before + j + 1)
                        for c in (2 * h, 2 * h + 1):
                            ins = act.activation(key_dif[:, c, :], iota[0:CE, w * WK:(w + 1) * WK], ACT.Identity,
                                                 bias=key_t[:, c, bass.ds(group, 1)], scale=-1.0)
                        ins.then_inc(s_dif[h], 1)

            def window_out(w):
                u = w % 2
                act.wait_ge(s_c, w + 1)
                act.activation(a_t[:, 0:T - 1, :, w * WD:(w + 1) * WD],
                               ps[u][:, 0, 0:(T - 1) * WK].rearrange("p (s d r) -> p s r d", s=T - 1, r=R),
                               ACT.Copy)
                act.activation(a_t[:, T - 1, :, w * WD:(w + 1) * WD],
                               ps[u][:, 1, 0:WK].rearrange("p (d r) -> p r d", r=R), ACT.Copy).then_inc(s_at, 1)
                for t in tiles_done(w):
                    h_out(t)

            for w in range(NW):
                window, window_next = window_next, next_regs(act, w, window_next)
                window_difs(w, window)
                if w == 0:
                    h_out(0)
                    h_out(1)
                else:
                    window_out(w - 1)
                if w in (1, 2):
                    unit_hi(2 + w)
                if w == NW - 2:
                    act.wait_ge(s_small, 32)
                    act.activation(rw_hl[:, :, 0, :], rw_sb[:, :, :], ACT.Copy).then_inc(s_rw, 1)
                    act.activation(ident_r[:, :], ident[:, :], ACT.Copy).then_inc(s_b1t, 1)
            window_out(NW - 1)
            def split_hi(pair, u):
                n = unit(pair, u)
                raw_v, hi_v, _ = unit_views(u)
                act.wait_ge(s_raw[w_slot(u)], 16 * ((n - w_slot(u)) // 2 + 1) if isinstance(pair, int)
                            else 16 * ((NG + u - w_slot(u)) // 2 + 1) + 32 * pair)
                if isinstance(pair, int) and pair == 0:
                    pass
                elif u < 2:
                    act.wait_ge(f_h, 2 * KH * pair)
                else:
                    act.wait_ge(f_y, 2 * T * pair)
                act.activation(hi_v, raw_v, ACT.Copy).then_inc(s_hi, 1)

            def rows_out(t):
                r = rows[t]
                act.wait_ge(s_ln, T + t + 1)
                if t >= 2:
                    act.wait_ge(s_xr, T + t - 1)
                act.activation(x3[t % 2][0:r, :], y_acc[0:r, t, :], ACT.Identity,
                               bias=nmr[0:r, t:t + 1], scale=rstd[0:r, t:t + 1]).then_inc(s_x3, 1)

            for s in range(T + 2):
                if 2 <= s != T:
                    rows_out(s - 2)
                t = s - 1
                if 0 <= t < T:
                    act.wait_ge(s_yt, t + 1)
                    if t >= 1:
                        act.wait_ge(s_o, t)
                    for k in range(KF):
                        ins = act.activation(yt_hl[0][0:frows[k], k, 0:rows[t]],
                                             ps[2 + t % 2][0:frows[k], 1, k * P:k * P + rows[t]], ACT.Copy)
                    ins.then_inc(s_yhi, 1)
                if s == T:
                    rows_out(s - 2)
                t = s - 2
                if 0 <= t < T:
                    split_rows(t, T + t)
                if s == T - 1:
                    split_hi(0, 0)
                if s < T:
                    r = rows[s]
                    act.wait_ge(s_m, s + 1)
                    act.activation(e_sb[0:r, :], m_sb[0:r, :], ACT.Exp).then_inc(s_e, 1)

            def hidden(pair, q, first_expert):
                hq = 2 * KH * pair + q
                act.wait_ge(f_h, hq + 1)
                act.wait_ge(f_lo, hq - 1) if not isinstance(hq, int) or hq >= 1 else None
                e = first_expert + q // KH
                col = b1_t[:, bass.ds(e * KH + q % KH, 1)] if not isinstance(e, int) else \
                    b1_t[:, e * KH + q % KH:e * KH + q % KH + 1]
                act.activation(g_sb[q % 2].rearrange("p (a n) -> p a n", a=2), hidden_bank(pair, q)[:, :, 0:NL],
                               ACT.Gelu, bias=col).then_inc(f_g, 1)

            def hidden_hi(pair, q):
                hq = 2 * KH * pair + q
                act.wait_ge(f_m, hq + 1)
                act.wait_ge(f_y, 2 * T * pair)
                act.activation(ht_hl[0][:, q, :], g_sb[q % 2], ACT.Copy).then_inc(f_hi, 1)

            def pair_act(pair, first_expert, last):
                if isinstance(pair, int) and pair == 0:
                    split_hi(0, 1)
                    act.wait_ge(s_gt, 1)
                    act.activation(g_t.rearrange("p (a n) -> p a n", a=2), ps[0][0:2 * NE, :, 0:NL],
                                   ACT.Copy).then_inc(s_gts, 1)
                split_hi(pair, 2)
                hidden(pair, 0, first_expert)
                hidden(pair, 1, first_expert)
                hidden_hi(pair, 0)
                hidden_hi(pair, 1)
                split_hi(pair, 3)
                if isinstance(pair, int) and pair == 0:
                    act.wait_ge(s_gd, 1)
                    act.activation(ge[:, :], gd[:, :], ACT.Exp).then_inc(s_ge, 1)
                hidden(pair, 2, first_expert)
                hidden(pair, 3, first_expert)
                hidden_hi(pair, 2)
                hidden_hi(pair, 3)
                if not last:
                    if isinstance(pair, int) and pair == 0:
                        for e in range(2):
                            wb_copy(e)
                    split_hi(pair + 1, 0)
                    if isinstance(pair, int) and pair == 0:
                        for e in range(2, 6):
                            wb_copy(e)
                    split_hi(pair + 1, 1)

            def wb_copy(e):
                act.wait_ge(s_wb, e + 1)
                act.activation(wb[:, e, 0:N + 1], wb_bank(e)[:, 0:N + 1], ACT.Copy).then_inc(s_wbs, 1)

            pair_act(0, NE, False)
            for e in range(6, NE):
                wb_copy(e)
            with act.Fori(0, NRP - 1) as i:
                pair_act(i + 1, 2 * i, False)
            pair_act(NRP, 2 * NRP - 2, True)

        @block.vector
        def _(dve):
            v = Tally(s_v)

            def step(ins):
                v.mark(ins)
                dve.wait_ge(s_v, v.n)

            dve.wait_ge(s_const, N_CONST)
            def stats(t, n, ready, value):
                r = rows[t]
                dve.wait_ge(ready, value)
                for h in range(2):
                    v.mark(dve.bn_stats(st[0:r, h, :], y_acc[0:r, t, h * 512:(h + 1) * 512]))
                dve.wait_ge(s_v, v.n)
                dve.bn_aggr(mv[0:r, t, :], st[0:r, :, :]).then_inc(s_mv, 1)
                dve.wait_ge(s_mv, n + 1)

            def split_rows_lo(t, n):
                dve.wait_ge(s_xhi, n + 1)
                cols = slice(t * P, t * P + rows[t])
                dve.tensor_tensor(xt[:, 1, :, cols], ps_rows(n)[:, :, 0:rows[t]],
                                  xt[:, 0, :, cols].bitcast(F32), ALU.subtract).then_inc(s_xlo, 1)

            def ranges():
                dve.wait_ge(s_kt, 1)
                dve.tensor_copy(key_t, ps[2][0:CE, 0, 0:CG * G].rearrange("p (j g) -> p j g", j=CG))
                step(dve.tensor_copy(src_t, ps[2][0:CE, 0, CG * G:2 * CG * G].rearrange("p (j g) -> p j g", j=CG)))
                kmin, kmax = ps[3][0:NW, 0, 0:G], ps[3][0:NW, 0, G:2 * G]
                step(dve.tensor_scalar(act_a, kmax, first_key[:, :], None, ALU.is_ge))
                step(dve.scalar_tensor_tensor(act_a, kmin, last_key[:, :], act_a, ALU.is_le, ALU.mult))
                step(dve.tensor_tensor(act_b, act_a, down, ALU.mult))
                step(dve.tensor_tensor(act_a, act_a, up, ALU.mult))
                step(dve.tensor_reduce(rng[:, 0:1], act_b, AX.X, ALU.max))
                step(dve.tensor_reduce(rng[:, 1:2], act_a, AX.X, ALU.max))
                step(dve.tensor_scalar(rng[:, 2:3], rng[:, 0:1], -1.0, float(G), ALU.mult, ALU.add))
                step(dve.tensor_scalar(rng[:, 2:3], rng[:, 2:3], float(G - H_PARTS), None, ALU.min))
                step(dve.tensor_tensor(rng[:, 3:4], rng[:, 1:2], rng[:, 2:3], ALU.subtract))
                dve.tensor_scalar(rng[:, 3:4], rng[:, 3:4], float(H_PARTS), None, ALU.max).then_inc(s_rng, 1)

            stats(0, 0, s_x[0], 16)
            dve.wait_ge(s_edge, 48)
            step(dve.scalar_tensor_tensor(key_f, dst_i, float(R), rel_i, ALU.mult, ALU.add))
            step(dve.tensor_copy(src_f, src_i))
            step(dve.tensor_reduce(kmm[:, 0:1], key_f, AX.X, ALU.min))
            step(dve.tensor_reduce(kmm[:, 1:2], key_f, AX.X, ALU.max))
            dve.tensor_copy(kmm_b[:, :, :], kmm[:, :].rearrange("p (a b) -> p a b", b=1)
                            .to_broadcast([G, 2, NW])).then_inc(s_kf, 1)
            stats(1, 1, s_x[1], 16)
            for s in range(1, T + 2):
                if s + 1 < T:
                    stats(s + 1, s + 1, s_x[s + 1], 16)
                if s in (3, 4):
                    unit_lo(dve, s - 3)
                t = s - 1
                if 0 <= t < T:
                    r = rows[t]
                    dve.wait_ge(s_rms, t + 1)
                    if t == 0:
                        dve.wait_ge(s_lnw, 16)
                    dve.scalar_tensor_tensor(xn[t % 2][0:r, :], h0[t % 2][0:r, :], rms[0:r, t:t + 1],
                                             lnw_row[0:r, :], ALU.mult, ALU.mult).then_inc(s_n, 1)
                t = s - 2
                if 0 <= t < T:
                    split_rows_lo(t, t)
                if s == 1:
                    ranges()
                if s == T - 1:
                    dve.wait_ge(s_win, 1)
                    window_next = next_regs(dve, -1)
                if s == 2:
                    dve.wait_ge(s_rt, 1)
                    dve.tensor_copy(win[:, :], ps[3][0:1, 1, 0:2 * NW]).then_inc(s_win, 1)

            def window_hots(window):
                first, number, before = window
                with dve.Fori(0, number) as j:
                    group = group_of(first, j)
                    for h in range(2):
                        dve.wait_ge(s_used[h], before + j + 1)
                        cs = slice(2 * h, 2 * h + 2)
                        dve.wait_ge(s_dif[h], before + j + 1)
                        dve.tensor_scalar(key_hot[:, cs, :], key_dif[:, cs, :], 0.0, None,
                                          ALU.is_equal).then_inc(s_eq[h], 1)
                        for c in (2 * h, 2 * h + 1):
                            ins = dve.tensor_scalar(src_hot[c], iota[0:CE, 0:NSRC],
                                                    src_t[:, c, bass.ds(group, 1)], None, ALU.is_equal)
                        ins.then_inc(s_hot[h], 1)

            for w in range(NW):
                window, window_next = window_next, next_regs(dve, w, window_next)
                window_hots(window)
            dve.wait_ge(s_rw, 1)
            dve.tensor_tensor(rw_hl[:, :, 1, :], rw_sb[:, :, :], rw_hl[:, :, 0, :].bitcast(F32),
                              ALU.subtract).then_inc(s_rw, 1)
            def split_lo(pair, u):
                raw_v, hi_v, lo_v = unit_views(u)
                dve.wait_ge(s_hi, unit(pair, u) + 1)
                dve.tensor_tensor(lo_v, raw_v, hi_v.bitcast(F32), ALU.subtract).then_inc(s_lo, 1)

            dve.wait_ge(s_convb, 16)
            for s in range(T + 2):
                t = s - 1
                if 0 <= t < T:
                    dve.wait_ge(s_yhi, t + 1)
                    for k in range(KF):
                        f, r = frows[k], rows[t]
                        ins = dve.tensor_tensor(yt_hl[1][0:f, k, 0:r], ps[2 + t % 2][0:f, 1, k * P:k * P + r],
                                                yt_hl[0][0:f, k, 0:r].bitcast(F32), ALU.subtract)
                    ins.then_inc(s_ylo, 1)
                t = s - 2
                if 0 <= t < T:
                    split_rows_lo(t, T + t)
                if s == T - 1:
                    split_lo(0, 0)
                if s < T:
                    r = rows[s]
                    dve.wait_ge(s_agg, s + 1)
                    if s >= 1:
                        dve.wait_ge(s_yt, s)
                    root_o, agg_o = agg_views(s)
                    for k in range(R):
                        v.mark(dve.tensor_scalar(cnt[0:r, k:k + 1], agg_o[k][-1][1][:, -1:], 1.0, None, ALU.max))
                    step(dve.tensor_tensor(z_sb[0:r, :], root_o, bias_row[0:r, :], ALU.add))
                    step(dve.reciprocal(inv[0:r, :], cnt[0:r, :]))
                    for k in range(R):
                        for at, o in agg_o[k]:
                            n = min(at + o.shape[1], F) - at
                            v.mark(dve.scalar_tensor_tensor(z_sb[0:r, at:at + n], o[:, 0:n], inv[0:r, k:k + 1],
                                                            z_sb[0:r, at:at + n], ALU.mult, ALU.add))
                        dve.wait_ge(s_v, v.n)
                    dve.tensor_scalar(m_sb[0:r, :], z_sb[0:r, :], 0.0, None, ALU.min).then_inc(s_m, 1)
                    step(dve.tensor_scalar(z_sb[0:r, :], z_sb[0:r, :], 0.0, None, ALU.max))
                    dve.wait_ge(s_e, s + 1)
                    dve.scalar_tensor_tensor(z_sb[0:r, :], e_sb[0:r, :], -1.0, z_sb[0:r, :],
                                             ALU.add, ALU.add).then_inc(s_y, 1)
                t = s - 1
                if 0 <= t < T:
                    r = rows[t]
                    dve.wait_ge(s_o, t + 1)
                    dve.wait_ge(s_xh, t + 1)
                    dve.tensor_tensor(y_acc[0:r, t, :], y_acc[0:r, t, :],
                                      ps[0][0:r, :, :].rearrange("p a n -> p (a n)"), ALU.add).then_inc(s_x2, 1)
                    stats(t, T + t, s_x2, t + 1)

            def route():
                dve.wait_ge(s_g, 1)
                for n in range(2):
                    for t in range(T):
                        r, c = rows[t], (2 * t + n) * NE
                        other = rb_row[0:r, :] if n == 0 else gate[0:r, t, :]
                        v.mark(dve.tensor_tensor(gate[0:r, t, :], ps[1][0:r, 0, c:c + NE], other, ALU.add))
                    dve.wait_ge(s_v, v.n)
                for t in range(T):
                    v.mark(dve.max(top[:, t, :], gate[:, t, :]))
                dve.wait_ge(s_v, v.n)
                for t in range(T):
                    v.mark(dve.max_index(top_i[:, t, :], top[:, t, :], gate[:, t, :]))
                dve.wait_ge(s_v, v.n)
                step(dve.tensor_tensor(gd[:, :], top[:, :, 1], top[:, :, 0], ALU.subtract))
                dve.tensor_copy(top_f[:, :, :], top_i[:, :, 0:2]).then_inc(s_gd, 1)
                dve.wait_ge(s_ge, 1)
                step(dve.tensor_scalar(gs[:, :], ge[:, :], 1.0, None, ALU.add))
                step(dve.reciprocal(pr[:, 0, :], gs[:, :]))
                step(dve.tensor_tensor(pr[:, 1, :], pr[:, 0, :], ge[:, :], ALU.mult))

                ei = e_idx[:, :].rearrange("p (a e) -> p a e", a=1).to_broadcast([P, T, NE])
                for j in range(2):
                    tf = top_f[:, :, j:j + 1].to_broadcast([P, T, NE])
                    pj = pr[:, j, :].rearrange("p (t a) -> p t a", a=1).to_broadcast([P, T, NE])
                    step(dve.tensor_tensor(hot[:, j], tf, ei, ALU.is_equal))
                    step(dve.tensor_tensor(hot[:, j], hot[:, j], pj, ALU.mult))
                step(dve.memset(w_sb[:, :, NE:NX], 1.0 / NS))
                dve.tensor_tensor(w_sb[:, :, 0:NE], hot[:, 0], hot[:, 1], ALU.add).then_inc(s_w, 1)
                dve.wait_ge(s_w, 1)
                step(dve.tensor_copy(w_hl[:, 0], w_sb[:, :, :]))
                dve.tensor_tensor(w_hl[:, 1], w_sb[:, :, :], w_hl[:, 0].bitcast(F32), ALU.subtract).then_inc(s_wr, 1)

            def hidden_scale(pair, q, e):
                hq = 2 * KH * pair + q
                dve.wait_ge(f_g, hq + 1)
                if e is None:
                    dve.tensor_scalar(g_sb[q % 2], g_sb[q % 2], 1.0 / NS, None, ALU.mult).then_inc(f_m, 1)
                else:
                    row = wb[:, bass.ds(e + q // KH, 1), :].rearrange("p a n -> p (a n)") \
                        if not isinstance(e, int) else wb[:, e + q // KH, :]
                    dve.tensor_tensor(g_sb[q % 2], g_sb[q % 2], row, ALU.mult).then_inc(f_m, 1)

            def hidden_lo(pair, q):
                hq = 2 * KH * pair + q
                dve.wait_ge(f_hi, hq + 1)
                dve.tensor_tensor(ht_hl[1][:, q, :], g_sb[q % 2], ht_hl[0][:, q, :].bitcast(F32),
                                  ALU.subtract).then_inc(f_lo, 1)

            def add_block(pair, b):
                t, h = block_of(b)
                n = 2 * T * pair + b
                dve.wait_ge(f_y, n + 1)
                dve.wait_ge(f_acc, n - 2 * T + 1) if not isinstance(pair, int) or pair > 0 else None
                dve.tensor_tensor(y_acc[0:rows[t], t, h * DH:(h + 1) * DH], y_acc[0:rows[t], t, h * DH:(h + 1) * DH],
                                  ps[2 + b % 4 // 2][0:rows[t], b % 2, :], ALU.add).then_inc(f_acc, 1)

            def pair_dve(pair, e, last):
                split_lo(pair, 2)
                for q in range(2):
                    hidden_scale(pair, q, e)
                for q in range(2):
                    hidden_lo(pair, q)
                if e is None:
                    route()
                split_lo(pair, 3)
                for q in range(2, 4):
                    hidden_scale(pair, q, e)
                for q in range(2, 4):
                    hidden_lo(pair, q)
                if e is None:
                    dve.wait_ge(s_wt, 1)
                    dve.tensor_copy(w_t[:, 0:N], ps[0][0:NX, :, :].rearrange("p a n -> p (a n)")[:, 0:N]) \
                       .then_inc(s_wts, 1)
                for b in range(2 * T):
                    add_block(pair, b)
                    if not last and b in (1, 4):
                        split_lo(pair + 1, b // 3)

            step(dve.memset(wb[:, :, N + 1:NP], 0.0))
            split_lo(0, 1)
            pair_dve(0, None, False)
            dve.wait_ge(s_wbs, NE)
            with dve.Fori(0, NRP - 1) as i:
                pair_dve(i + 1, 2 * i, False)
            pair_dve(NRP, 2 * NRP - 2, True)

        @block.tensor
        def _(pe):
            def hilo(out_ap, parts, start=True, stop=True):
                n = 3 * len(parts)
                k = 0
                for (lh, ll), (rh, rl) in parts:
                    for a, b in ((lh, rh), (lh, rl), (ll, rh)):
                        ins = pe.matmul(out_ap, a, b, start=start and k == 0, stop=stop and k == n - 1)
                        k += 1
                return ins

            for used in (*s_used, *s_eq):
                pe.sem_inc(used, 1)
            pe.wait_ge(s_const, N_CONST)
            pe.wait_ge(s_kf, 1)
            for n, v in enumerate((key_f, src_f)):
                for j in range(CG):
                    c = (CG * n + j) * G
                    pe.transpose(ps[2][0:CE, 0, c:c + G], v[:, j * CE:(j + 1) * CE], ident[0:G, 0:G])
            for n in range(2):
                ins = pe.matmul(ps[3][0:NW, 0, n * G:(n + 1) * G], kmm_b[:, n, :], ident[0:G, 0:G],
                                start=True, stop=True)
            ins.then_inc(s_kt, 1)
            pe.wait_ge(s_b1, 32)
            pe.transpose(ps[2][:, 1, 0:NX * KH], b1_rows[:, :], ident[0:NX * KH, 0:NX * KH]).then_inc(s_bt, 1)

            def rows_t(source, ready, t, n):
                pe.wait_ge(ready, t + 1)
                if n >= 2:
                    pe.wait_ge(s_xlo, n - 1 if n < T else n)
                for k in range(KD):
                    ins = pe.transpose(ps_rows(n)[:, k, 0:rows[t]], source[t % 2][0:rows[t], k * P:(k + 1) * P],
                                       ident[0:rows[t], 0:rows[t]])
                ins.then_inc(s_xr, 1)

            for t in range(2):
                rows_t(xn, s_n, t, t)
            pe.wait_ge(s_rng, 1)
            pe.matmul(ps[3][0:1, 1, 0:NW], rng[:, 2:3], ident[0:NW, 0:NW], start=True, stop=True)
            pe.matmul(ps[3][0:1, 1, NW:2 * NW], rng[:, 3:4], ident[0:NW, 0:NW],
                      start=True, stop=True).then_inc(s_rt, 1)
            def project(t, r):
                cols = slice(t * P, t * P + rows[t])
                return hilo(ps[h_bank(t)][0:rows[t], r, 0:F],
                            [((xt[:, 0, k, cols], xt[:, 1, k, cols]), (rel_hl[0][:, r, k], rel_hl[1][:, r, k]))
                             for k in range(KD)])

            for t in range(2, T):
                rows_t(xn, s_n, t, t)
                if t == T - 1:
                    window_next = next_regs(pe, -1, None, False)
                if t >= 3:
                    pe.wait_ge(s_xlo, t - 2)
                    if t == 3:
                        pe.wait_ge(s_win, 1)
                        pe.wait_ge(s_lo, R)
                    else:
                        pe.wait_ge(s_b1t, 1)
                    for r in range(R):
                        ins = project(t - 3, r)
                    ins.then_inc(s_h, 1)
            pe.wait_ge(s_xlo, T)

            def h_part(w, part):
                if not 1 <= w <= NW - 2:
                    return
                for t, r, k in steps_of(H_PARTS * (w - 1) + part):
                    if r == 0 and k == 0:
                        pe.wait_ge(s_hs, t - 1)
                    cols = slice(t * P, t * P + rows[t])
                    ins = hilo(ps[h_bank(t)][0:rows[t], r, 0:F],
                               [((xt[:, 0, k, cols], xt[:, 1, k, cols]), (rel_hl[0][:, r, k], rel_hl[1][:, r, k]))],
                               start=k == 0, stop=k == KD - 1)
                    if r == R - 1 and k == KD - 1:
                        ins.then_inc(s_h, 1)

            def window_counts(w, window):
                first, number, before = window
                u = w % 2
                if w >= 2:
                    pe.wait_ge(s_at, w - 1)
                full, last = ps[u][:, 0, 0:(T - 1) * WK], ps[u][:, 1, 0:WK]
                for o in (full, last):
                    pe.matmul(o, zeros[:, 0:P], zeros[:, 0:o.shape[1]], start=True, stop=False)

                def group(j):
                    for h in range(2):
                        pe.wait_ge(s_hot[h], before + j + 1)
                        for c in (2 * h, 2 * h + 1):
                            for s in range(T):
                                o = full[:, s * WK:(s + 1) * WK] if s < T - 1 else last
                                ins = pe.matmul(o, src_hot[c][:, s * P:(s + 1) * P], key_hot[:, c, :],
                                                start=False, stop=False)
                        ins.then_inc(s_used[h], 1)

                at = 0
                for part in range(H_PARTS):
                    end = number * (part + 1) // H_PARTS if part + 1 < H_PARTS else number
                    with pe.Fori(at, end) as j:
                        group(j)
                    if part + 1 < H_PARTS:
                        h_part(w, part)
                    at = end
                for o in (full, last):
                    ins = pe.matmul(o, zeros[:, 0:P], zeros[:, 0:o.shape[1]], start=False, stop=True)
                ins.then_inc(s_c, 1)

            for w in range(NW):
                window, window_next = window_next, next_regs(pe, w, window_next, False)
                window_counts(w, window)
                h_part(w, H_PARTS - 1)

            def root(t, whole=True):
                if t >= 2:
                    pe.wait_ge(s_ylo, t - 1)
                cols = slice(t * P, t * P + rows[t])
                hilo(agg_views(t)[0], [((xt[:, 0, k, cols], xt[:, 1, k, cols]), (root_hl[0][:, k], root_hl[1][:, k]))
                                       for k in range(KD)], start=whole, stop=whole)

            def aggregate(t, r, tiles, start=True, stop=True):
                cols = slice(t * P, t * P + rows[t])
                for at, o in agg_views(t)[1][r]:
                    for s in tiles:
                        ins = pe.matmul(o, a_t[0:rows[s], s, r, cols], h_rel[s][0:rows[s], r, at:at + o.shape[1]],
                                        start=start and s == tiles[0], stop=stop and s == tiles[-1])
                return ins

            def elu_t(t):
                pe.wait_ge(s_y, t + 1)
                for k in range(KF):
                    ins = pe.transpose(ps[2 + t % 2][0:frows[k], 1, k * P:k * P + rows[t]],
                                       z_sb[0:rows[t], k * FK:k * FK + frows[k]], ident[0:rows[t], 0:rows[t]])
                ins.then_inc(s_yt, 1)

            def output(t):
                pe.wait_ge(s_ylo, t + 1)
                if t >= 1:
                    pe.wait_ge(s_x2, t)
                for h in range(2):
                    ins = hilo(ps[0][0:rows[t], h, :],
                               [((yt_hl[0][0:frows[k], k, 0:rows[t]], yt_hl[1][0:frows[k], k, 0:rows[t]]),
                                 (wo_hl[0][0:frows[k], k, h * DH:(h + 1) * DH],
                                  wo_hl[1][0:frows[k], k, h * DH:(h + 1) * DH])) for k in range(KF)])
                ins.then_inc(s_o, 1)

            def gates(a):
                for k in range(KD):
                    for n in range(2):
                        ins = pe.matmul(ps[0][0:2 * NE, a, 0:NL], rw_hl[:, k, :, :].rearrange("p a e -> p (a e)"),
                                        xt[:, n, k, a * NL:(a + 1) * NL],
                                        start=(k == 0 and n == 0), stop=(k == KD - 1 and n == 1))
                return ins

            def up_half(pair, e, m, a):
                return hilo(hidden_bank(pair, KH * e + m)[:, a, 0:NL],
                            [((w1_hl[0][:, e, k, m * P:(m + 1) * P], w1_hl[1][:, e, k, m * P:(m + 1) * P]),
                              (xt[:, 0, k, a * NL:(a + 1) * NL], xt[:, 1, k, a * NL:(a + 1) * NL]))
                             for k in range(KD)])

            pe.wait_ge(s_lo, NG)
            pe.wait_ge(s_at, NW)
            pe.wait_ge(s_hs, T)
            pe.wait_ge(s_ones, T)
            slot0, slot1 = (0, 1, 2), (3, 4)
            for s in range(T - 1):
                root(s)
                aggregate(s, 0, slot0 + slot1)
                if s >= 1:
                    elu_t(s - 1)
                if s >= 2:
                    rows_t(x3, s_x3, s - 2, T + s - 2)
                aggregate(s, 1, slot0 + slot1).then_inc(s_agg, 1)
                if s >= 1:
                    output(s - 1)
            pe.wait_ge(s_ylo, T - 2)
            banks = [ps[2 + (T - 1) % 2][0:rows[-1], a, :] for a in range(2)]
            for bank in banks:
                pe.matmul(bank, zeros[:, 0:rows[-1]], zeros[:, :], start=True, stop=False)
            for r in range(R):
                ins = aggregate(T - 1, r, slot1, start=False, stop=False)
            ins.then_inc(s_slot1, 1)
            root(T - 1, whole=False)
            aggregate(T - 1, 0, slot0, start=False, stop=False)
            elu_t(T - 2)
            rows_t(x3, s_x3, T - 3, 2 * T - 3)
            aggregate(T - 1, 1, slot0, start=False, stop=False)
            for bank in banks:
                ins = pe.matmul(bank, zeros[:, 0:rows[-1]], zeros[:, :], start=False, stop=True)
            ins.then_inc(s_agg, 1)
            output(T - 2)
            assert NL <= (T - 2) * P
            pe.wait_ge(s_xlo, 2 * T - 2)
            pe.wait_ge(s_lo, unit(0, 0) + 1)
            up_half(0, 0, 0, 0)
            elu_t(T - 1)
            output(T - 1)
            rows_t(x3, s_x3, T - 2, 2 * T - 2)
            up_half(0, 0, 1, 0)
            pe.wait_ge(s_rw, 2)
            pe.wait_ge(s_x2, T)
            gates(0)
            rows_t(x3, s_x3, T - 1, 2 * T - 1)
            pe.wait_ge(s_xlo, 2 * T)
            gates(1).then_inc(s_gt, 1)
            for m in range(KH):
                up_half(0, 0, m, 1).then_inc(f_h, 1)
            pe.wait_ge(s_gts, 1)
            for t in range(T):
                ins = pe.transpose(ps[1][0:rows[t], 0, 2 * t * NE:2 * (t + 1) * NE],
                                   g_t[:, t * P:t * P + rows[t]], ident[0:2 * NE, 0:2 * NE])
            ins.then_inc(s_g, 1)

            def up_expert(pair, e):
                pe.wait_ge(s_lo, unit(pair, e) + 1)
                for m in range(KH):
                    q = KH * e + m
                    hq = 2 * KH * pair + q
                    if not isinstance(pair, int):
                        pe.wait_ge(f_g, hq - 1)
                    elif m == 1:
                        pe.wait_ge(s_gd, 1)
                    for a in range(2):
                        ins = up_half(pair, e, m, a)
                    ins.then_inc(f_h, 1)

            def down_pair(pair, bias):
                def part(b, experts, start, stop):
                    t, h = block_of(b)
                    cols = slice(t * P, t * P + rows[t])
                    return hilo(ps[2 + b % 4 // 2][0:rows[t], b % 2, :],
                                [((ht_hl[0][:, KH * e + m, cols], ht_hl[1][:, KH * e + m, cols]),
                                  (w2_hl[0][:, e, m, h * DH:(h + 1) * DH], w2_hl[1][:, e, m, h * DH:(h + 1) * DH]))
                                 for e in experts for m in range(KH)], start=start, stop=stop)

                def opened(b):
                    n = 2 * T * pair + b
                    if not isinstance(n, int) or n >= 4:
                        pe.wait_ge(f_acc, n - 1 if b < 2 else n - 3)
                    return True

                pe.wait_ge(s_lo, unit(pair, 2) + 1)
                pe.wait_ge(f_lo, 2 * KH * pair + KH)
                if bias:
                    pe.wait_ge(f_g, KH)
                for b in range(4):
                    part(b, (0,), opened(b), False)
                if bias:
                    pe.wait_ge(s_w, 1)
                    pe.wait_ge(f_g, 2 * KH)
                    for t in range(T):
                        ins = pe.transpose(ps[0][:, :, :].rearrange("p a n -> p (a n)")
                                           [0:NX, t * P:t * P + rows[t]],
                                           w_sb[0:rows[t], t, :], ident[0:rows[t], 0:rows[t]])
                    ins.then_inc(s_wt, 1)
                pe.wait_ge(s_lo, unit(pair, 3) + 1)
                pe.wait_ge(f_lo, 2 * KH * pair + 2 * KH)
                for b in range(2 * T):
                    ins = part(b, (1,) if b < 4 else (0, 1), b >= 4 and opened(b), not bias)
                    if bias:
                        t, h = block_of(b)
                        if b == 0:
                            pe.wait_ge(s_wts, 1)
                            pe.wait_ge(s_b2, 32)
                        ins = pe.matmul(ps[2 + b % 4 // 2][0:rows[t], b % 2, :], w_t[:, t * P:t * P + rows[t]],
                                        b2_sb[:, h * DH:(h + 1) * DH], start=False, stop=True)
                    ins.then_inc(f_y, 1)
                    if bias and 1 <= b <= NE:
                        spread(b - 1)

            def spread(e):
                if e == 0:
                    pe.wait_ge(s_wr, 1)
                    pe.wait_ge(s_b1t, 2)
                if e >= 2:
                    pe.wait_ge(s_wbs, e - 1)
                for t in range(T):
                    n = rows[t] + rows[t] % 2
                    for h in range(2):
                        ins = pe.matmul(wb_bank(e)[:, t * P:t * P + n],
                                        w_hl[0:rows[t], h, t, e:e + 1].to_broadcast([rows[t], P]),
                                        ident_r[0:rows[t], 0:n], start=(h == 0), stop=(h == 1))
                ins.then_inc(s_wb, 1)

            def pair_pe(pair):
                up_expert(pair, 0)
                up_expert(pair, 1)
                down_pair(pair, False)

            up_expert(0, 1)
            down_pair(0, True)
            pe.wait_ge(s_wbs, NE)
            with pe.Fori(0, NRP) as i:
                pair_pe(i + 1)
    return nc


INS = ["x", "src", "dst", "edge_type_2", "L0_gnn_ln_weight", "L0_gnn_W_rel", "L0_gnn_W_root", "L0_gnn_conv_bias",
       "L0_gnn_wo_weight", "L0_ffn_rW", "L0_ffn_rb", "L0_ffn_W1", "L0_ffn_b1", "L0_ffn_W2", "L0_ffn_b2",
       "L0_ffn_sW1", "L0_ffn_sb1", "L0_ffn_sW2", "L0_ffn_sb2"]


def kernel(**inputs):
    import numpy as np
    import concourse.bacc as bacc
    from concourse.bass_utils import run_bass_kernel_spmd

    nc = bacc.Bacc("TRN2", target_bir_lowering=False, num_devices=1)
    arrays, args = {}, []
    for name in INS:
        a = np.ascontiguousarray(inputs[name])
        arrays[f"in_{name}"] = a
        args.append(nc.dram_tensor(f"in_{name}", a.shape, mybir.dt.from_np(a.dtype), kind="ExternalInput").ap())
    out = nc.dram_tensor("out", inputs["x"].shape, F32, kind="ExternalOutput").ap()
    program(nc, *args, out)
    return run_bass_kernel_spmd(nc, [arrays], core_ids=[0]).results[0]["out"]
```
